# Optimizing a Trainium2 kernel written in Bass

```python
import numpy as np
import jax
import jax.numpy as jnp

def _softmax(x, axis=-1):
    return jax.nn.softmax(x, axis=axis)

def _gelu(x):
    return jax.nn.gelu(x, approximate=True)

def _silu(x):
    return jax.nn.silu(x)

def _sigmoid(x):
    return jax.nn.sigmoid(x)

def _layernorm(x, axis=-1, eps=1e-05):
    m = jnp.mean(x, axis=axis, keepdims=True)
    v = jnp.var(x, axis=axis, keepdims=True)
    return (x - m) / jnp.sqrt(v + eps)

def _scatter_add(tgt, idx, src, axis=0):
    return tgt.at[idx].add(src)

def _segment_sum(src, seg, n):
    return jax.ops.segment_sum(src, seg, n)
kernel_name = 'mk_xattn_ffn_d1_seqx_r2_706ed8'

def setup_inputs(seed: int=0):
    np.random.seed(seed)
    _w = jnp.asarray

    def _rec_inputs():
        import jax
        import jax.numpy as jnp
        _rk = jax.random.key(seed)
        x = -0.0002928 + 1 * jax.random.normal(jax.random.fold_in(_rk, 1), (8, 1024, 512), jnp.float32)
        _lenS = 1024 - jax.random.randint(jax.random.fold_in(_rk, 7), (8,), 0, max(1, 1024 // 4) + 1, jnp.int32)
        _lenS2 = 1024 - jax.random.randint(jax.random.fold_in(_rk, 8), (8,), 0, max(1, 1024 // 4) + 1, jnp.int32)
        _ctx_1024P = jax.random.normal(jax.random.fold_in(_rk, 11), (8, 16, 512), jnp.float32)
        _ctx_1024c = jax.random.dirichlet(jax.random.fold_in(_rk, 511), 0.3 * jnp.ones((16,), jnp.float32), (8, 1024))
        _ctx_1024t = jnp.einsum('bsk,bkd->bsd', _ctx_1024c, _ctx_1024P)
        _ctx_1024t = _ctx_1024t * jax.lax.rsqrt(jnp.mean(jnp.square(_ctx_1024t)) + 1e-12) * 0.953939
        ctx_1024 = -1.39393e-06 + 0.999914 * (_ctx_1024t + 0.3 * jax.random.normal(jax.random.fold_in(_rk, 611), (8, 1024, 512), jnp.float32))
        return (x, ctx_1024)
    x, ctx_1024 = _rec_inputs()

    def _L0_xattn_setup():
        import jax, jax.numpy as jnp
        import numpy as np
        B, S, D, NH = (2, 1024, 512, 8)
        DH = D // NH
        EPS = 1e-06
        LN_EPS = 1e-05

        def _mlstm_cell(q, k, v, igate_w, igate_b, fgate_w, fgate_b, ln_scale):
            Slen = q.shape[0]
            ifg = jnp.concatenate([q, k, v], axis=-1)
            ig = (ifg @ igate_w.T + igate_b).T
            fg = (ifg @ fgate_w.T + fgate_b).T
            qh = q.reshape(Slen, NH, DH).transpose(1, 0, 2)
            kh = k.reshape(Slen, NH, DH).transpose(1, 0, 2)
            vh = v.reshape(Slen, NH, DH).transpose(1, 0, 2)
            log_f = jax.nn.log_sigmoid(fg)
            cs = jnp.cumsum(log_f, axis=1)
            fg_mat = cs[:, :, None] - cs[:, None, :]
            mask = jnp.tril(jnp.ones((Slen, Slen), dtype=bool))
            log_fg_mat = jnp.where(mask, fg_mat, -jnp.inf)
            log_D = log_fg_mat + ig[:, None, :]
            max_log_D = jnp.max(log_D, axis=-1, keepdims=True)
            D_mat = jnp.exp(log_D - max_log_D)
            qk = jnp.einsum('hsd,htd->hst', qh, kh) / np.sqrt(DH)
            C = qk * D_mat
            normalizer = jnp.maximum(jnp.abs(C.sum(axis=-1, keepdims=True)), jnp.exp(-max_log_D))
            h = jnp.einsum('hst,htd->hsd', C / (normalizer + EPS), vh)
            h = h.transpose(1, 0, 2).reshape(Slen, D)
            mu = h.mean(axis=-1, keepdims=True)
            var = h.var(axis=-1, keepdims=True)
            return (h - mu) / jnp.sqrt(var + LN_EPS) * ln_scale
        key = jax.random.key(seed)
        ks = jax.random.split(key, 8)
        rnd = lambda k, sh, s=1.0: jax.random.normal(k, sh, dtype=jnp.float32) * s
        return {'q': rnd(ks[0], (B, S, D)), 'k': rnd(ks[1], (B, S, D)), 'v': rnd(ks[2], (B, S, D)), 'igate_w': rnd(ks[3], (NH, 3 * D), 0.02), 'igate_b': jnp.linspace(3.0, 6.0, NH, dtype=jnp.float32), 'fgate_w': rnd(ks[4], (NH, 3 * D), 0.02), 'fgate_b': rnd(ks[5], (NH,), 0.3162278), 'ln_scale': jnp.ones((D,), dtype=jnp.float32)}
    _L0_xattn_all = _L0_xattn_setup()
    _L0_xattn_in = {k: v for k, v in _L0_xattn_all.items() if k in ('igate_w', 'igate_b', 'fgate_w', 'fgate_b', 'ln_scale')}
    del _L0_xattn_all

    def _L0_ffn_setup():
        import jax, jax.numpy as jnp
        import numpy as np
        B, S, H, F, G = (8, 1024, 512, 2048, 128)
        EPS = 1e-05

        def _dequant(q, scales, g):
            K, N = q.shape
            w = (q.astype(jnp.float32) - 128.0).reshape(K // g, g, N) * scales[:, None, :]
            return w.reshape(K, N)
        key = jax.random.key(seed)
        ks = jax.random.split(key, 8)
        x = jax.random.normal(ks[0], (B, S, H), dtype=jnp.float32)
        ln_gamma = jnp.ones((H,), jnp.float32)
        ln_beta = jnp.zeros((H,), jnp.float32)
        fc1_q = jax.random.randint(ks[1], (H, F), 0, 128, dtype=jnp.int32)
        fc2_q = jax.random.randint(ks[2], (F, H), 0, 128, dtype=jnp.int32)
        fc1_scales = jax.random.uniform(ks[3], (H // G, F), jnp.float32) * 0.02 + 0.001
        fc2_scales = jax.random.uniform(ks[4], (F // G, H), jnp.float32) * 0.02 + 0.001
        fc1_bias = jax.random.normal(ks[5], (F,), jnp.float32) * 0.02
        fc2_bias = jax.random.normal(ks[6], (H,), jnp.float32) * 0.02
        return {'x': x, 'ln_gamma': ln_gamma, 'ln_beta': ln_beta, 'fc1_q': fc1_q, 'fc1_scales': fc1_scales, 'fc1_bias': fc1_bias, 'fc2_q': fc2_q, 'fc2_scales': fc2_scales, 'fc2_bias': fc2_bias}
    _L0_ffn_all = _L0_ffn_setup()
    _L0_ffn_in = {k: v for k, v in _L0_ffn_all.items() if k in ('ln_gamma', 'ln_beta', 'fc1_q', 'fc1_scales', 'fc1_bias', 'fc2_q', 'fc2_scales', 'fc2_bias')}
    del _L0_ffn_all
    return {'x': x, 'ctx_1024': ctx_1024, 'L0_xattn_igate_w': _L0_xattn_in['igate_w'], 'L0_xattn_igate_b': _L0_xattn_in['igate_b'], 'L0_xattn_fgate_w': _L0_xattn_in['fgate_w'], 'L0_xattn_fgate_b': _L0_xattn_in['fgate_b'], 'L0_xattn_ln_scale': _L0_xattn_in['ln_scale'], 'L0_ffn_ln_gamma': _L0_ffn_in['ln_gamma'], 'L0_ffn_ln_beta': _L0_ffn_in['ln_beta'], 'L0_ffn_fc1_q': _L0_ffn_in['fc1_q'], 'L0_ffn_fc1_scales': _L0_ffn_in['fc1_scales'], 'L0_ffn_fc1_bias': _L0_ffn_in['fc1_bias'], 'L0_ffn_fc2_q': _L0_ffn_in['fc2_q'], 'L0_ffn_fc2_scales': _L0_ffn_in['fc2_scales'], 'L0_ffn_fc2_bias': _L0_ffn_in['fc2_bias']}

def reference(x, ctx_1024, L0_xattn_igate_w, L0_xattn_igate_b, L0_xattn_fgate_w, L0_xattn_fgate_b, L0_xattn_ln_scale, L0_ffn_ln_gamma, L0_ffn_ln_beta, L0_ffn_fc1_q, L0_ffn_fc1_scales, L0_ffn_fc1_bias, L0_ffn_fc2_q, L0_ffn_fc2_scales, L0_ffn_fc2_bias):
    import jax
    import jax.numpy as jnp

    def _L0_xattn_ref(q, k, v, igate_w, igate_b, fgate_w, fgate_b, ln_scale):
        import jax, jax.numpy as jnp
        import numpy as np
        B, S, D, NH = (2, 1024, 512, 8)
        DH = D // NH
        EPS = 1e-06
        LN_EPS = 1e-05

        def _mlstm_cell(q, k, v, igate_w, igate_b, fgate_w, fgate_b, ln_scale):
            Slen = q.shape[0]
            ifg = jnp.concatenate([q, k, v], axis=-1)
            ig = (ifg @ igate_w.T + igate_b).T
            fg = (ifg @ fgate_w.T + fgate_b).T
            qh = q.reshape(Slen, NH, DH).transpose(1, 0, 2)
            kh = k.reshape(Slen, NH, DH).transpose(1, 0, 2)
            vh = v.reshape(Slen, NH, DH).transpose(1, 0, 2)
            log_f = jax.nn.log_sigmoid(fg)
            cs = jnp.cumsum(log_f, axis=1)
            fg_mat = cs[:, :, None] - cs[:, None, :]
            mask = jnp.tril(jnp.ones((Slen, Slen), dtype=bool))
            log_fg_mat = jnp.where(mask, fg_mat, -jnp.inf)
            log_D = log_fg_mat + ig[:, None, :]
            max_log_D = jnp.max(log_D, axis=-1, keepdims=True)
            D_mat = jnp.exp(log_D - max_log_D)
            qk = jnp.einsum('hsd,htd->hst', qh, kh) / np.sqrt(DH)
            C = qk * D_mat
            normalizer = jnp.maximum(jnp.abs(C.sum(axis=-1, keepdims=True)), jnp.exp(-max_log_D))
            h = jnp.einsum('hst,htd->hsd', C / (normalizer + EPS), vh)
            h = h.transpose(1, 0, 2).reshape(Slen, D)
            mu = h.mean(axis=-1, keepdims=True)
            var = h.var(axis=-1, keepdims=True)
            return (h - mu) / jnp.sqrt(var + LN_EPS) * ln_scale
        return jax.vmap(lambda qq, kk, vv: _mlstm_cell(qq, kk, vv, igate_w, igate_b, fgate_w, fgate_b, ln_scale))(q, k, v)

    def _L0_ffn_ref(x, ln_gamma, ln_beta, fc1_q, fc1_scales, fc1_bias, fc2_q, fc2_scales, fc2_bias):
        import jax, jax.numpy as jnp
        import numpy as np
        B, S, H, F, G = (8, 1024, 512, 2048, 128)
        EPS = 1e-05

        def _dequant(q, scales, g):
            K, N = q.shape
            w = (q.astype(jnp.float32) - 128.0).reshape(K // g, g, N) * scales[:, None, :]
            return w.reshape(K, N)
        residual = x
        mu = jnp.mean(x, axis=-1, keepdims=True)
        var = jnp.mean(jnp.square(x - mu), axis=-1, keepdims=True)
        h = (x - mu) * jax.lax.rsqrt(var + EPS) * ln_gamma + ln_beta
        hf = h.reshape(-1, H)
        w1 = _dequant(fc1_q, fc1_scales, G)
        y = hf @ w1 + fc1_bias
        y = jax.nn.silu(y)
        w2 = _dequant(fc2_q, fc2_scales, G)
        z = y @ w2 + fc2_bias
        return residual + 0.5 * z.reshape(residual.shape)
    x = x + _L0_xattn_ref(_layernorm(x, axis=-1), ctx_1024, ctx_1024, L0_xattn_igate_w, L0_xattn_igate_b, L0_xattn_fgate_w, L0_xattn_fgate_b, L0_xattn_ln_scale)
    x = x + _L0_ffn_ref(_layernorm(x, axis=-1), L0_ffn_ln_gamma, L0_ffn_ln_beta, L0_ffn_fc1_q, L0_ffn_fc1_scales, L0_ffn_fc1_bias, L0_ffn_fc2_q, L0_ffn_fc2_scales, L0_ffn_fc2_bias)
    return x

_drawn_inputs = setup_inputs


def setup_inputs(seed=0):
    import zlib

    import numpy as np

    out = dict(_drawn_inputs(seed))
    spreads = {'L0_xattn_ln_scale': (1.0, 0.2),
     'L0_ffn_ln_gamma': (1.0, 0.2),
     'L0_ffn_ln_beta': (0.0, 0.1)}
    factors = {}
    for name, (base, spread) in spreads.items():
        noise = np.random.default_rng([zlib.crc32(name.encode()), seed]).standard_normal(out[name].shape)
        drawn = base * np.exp(spread * noise) if base else spread * noise
        out[name] = jnp.asarray(drawn.astype(out[name].dtype))
    for name, factor in factors.items():
        out[name] = (out[name] * factor).astype(out[name].dtype)
    return out
```

```python
from contextlib import ExitStack

import concourse.bass as bass
from concourse import mybir

P = 128
ALU = mybir.AluOpType
ACT = mybir.ActivationFunctionType
F32 = mybir.dt.float32
F32R = mybir.dt.float32r
I32 = mybir.dt.int32

LN_EPS = 1e-5
NORM_EPS = 1e-6
NEG = -1e30
LAG = 5


def build(nc, x, ctx, igate_w, igate_b, fgate_w, fgate_b, ln_scale, gamma, beta,
          q1, s1, b1, q2, s2, b2, out):
    B, S, D = x.shape
    NH = igate_w.shape[0]
    DH = D // NH
    PR = NH // 2
    KT = D // P
    F = q1.shape[1]
    NJ = F // P
    CB = S // P
    NG = B * CB
    HC = 4
    R = HC * P
    NU = NJ * NG // HC
    UB = NJ * CB // HC
    UPS = NJ // HC
    VW = DH + 1
    assert KT == PR and DH * 2 == P and UPS == 4

    xf = x.rearrange("b s d -> (b s) d")
    cf = ctx.rearrange("b s d -> (b s) d")
    of = out.rearrange("b s d -> (b s) d")
    resid = nc.dram_tensor("resid_scratch", [NG * P, D], F32, kind="Internal").ap()

    with ExitStack() as es:
        def sb(name, shape, dt=F32):
            return es.enter_context(nc.sbuf_tensor(name, shape, dt))

        def pb(name):
            return es.enter_context(nc.psum_tensor(name, [P, 512], F32))

        def sem(name):
            return es.enter_context(nc.semaphore(name))

        w1h = sb("w1h", [P, KT, F], F32R)
        w1l = sb("w1l", [P, KT, F], F32R)
        w2h = sb("w2h", [P, NJ, D], F32R)
        w2l = sb("w2l", [P, NJ, D], F32R)
        hstage = sb("hstage", [P, KT, R])
        hhi = sb("hhi", [P, KT, R], F32R)
        hlo = sb("hlo", [P, KT, R], F32R)
        ybuf = sb("ybuf", [P, 2, R])
        tbuf = sb("tbuf", [P, R])
        yhi = sb("yhi", [P, 2, R], F32R)
        ylo = sb("ylo", [P, 2, R], F32R)
        rin = sb("rin", [P, HC, D])
        xin = sb("xin", [P, 2, D])
        vaug = sb("vaug", [P, 2, PR, 2 * VW])
        qn = sb("qn", [P, D])
        kg_u = sb("kg_u", [P, D])
        qT = sb("qT", [P, PR, P])
        kT = sb("kT", [P, PR, P])
        qpT = sb("qpT", [P, PR, P])
        dmat = sb("dmat", [P, 2, PR, P])
        hx = sb("hx", [P, D])
        state = sb("state", [P, PR, VW])
        ident = sb("ident", [P, P])
        tri = sb("tri", [P, P])
        ones = sb("ones", [P, 1])
        lnsc = sb("lnsc", [P, D])
        b2h = sb("b2h", [P, D])
        wg = sb("wg", [P, 2 * KT, 2 * NH])
        gbias = sb("gbias", [P, 2 * NH])
        gbraw = sb("gbraw", [P, 2 * NH])
        gcol = sb("gcol", [P, KT])
        bcol = sb("bcol", [P, KT])
        b1c = sb("b1c", [P, NJ])
        b1h = sb("b1h", [P, NJ])
        neghalf = sb("neghalf", [P, 1])
        minit = sb("minit", [P, NH])
        sel = sb("sel", [40, NH], F32R)
        sel32 = sb("sel32", [40, NH])
        at = sb("at", [NH, 2, P])
        ats = sb("ats", [40, P], F32R)
        xst = sb("xst", [P, 6])
        xmv = sb("xmv", [P, 4])
        hst = sb("hst", [P, 6])
        hmv = sb("hmv", [P, 4])
        ost = sb("ost", [P, 6])
        omv = sb("omv", [P, 8])
        gate = sb("gate", [P, 2 * NH])
        gtmp = sb("gtmp", [P, 3, NH])
        lf = sb("lf", [P, NH])
        lfsum = sb("lfsum", [P, NH])
        cs = sb("cs", [P, NH])
        acol = sb("acol", [P, NH])
        an = sb("an", [P, NH])
        mnew = sb("mnew", [P, 2, NH])
        ex = sb("ex", [P, 4, NH])
        fac = sb("fac", [P, 4, NH])
        nrm = sb("nrm", [P, 2, NH])
        gwraw = hstage[0:2 * NH, :, :].rearrange("p a b -> p (a b)")[:, 0:3 * D]

        bankA, bankB = pb("bankA"), pb("bankB")
        ypsum = [pb("ypsum0"), pb("ypsum1")]
        zpsum = [pb(f"zpsum{m}") for m in range(HC)]

        l_const, l_gw, l_bias = sem("l_const"), sem("l_gw"), sem("l_bias")
        l_q = [sem("l_q0"), sem("l_q1")]
        l_s = [sem("l_s0"), sem("l_s1")]
        l_x = [sem("l_x0"), sem("l_x1")]
        l_ctx = [sem("l_ctx0"), sem("l_ctx1")]
        l_rin = [sem(f"l_rin{m}") for m in range(HC)]
        st_r = sem("st_r")
        rin_left = [sem(f"rin_left{m}") for m in range(HC)]
        c_zero, c_ident, c_gwT, c_ready = sem("c_zero"), sem("c_ident"), sem("c_gwT"), sem("c_ready")
        c_sel, c_gcopy, c_wg, c_dve = sem("c_sel"), sem("c_gcopy"), sem("c_wg"), sem("c_dve")
        w_raw, w_hi, w_lo, w_bias, c_b1 = sem("w_raw"), sem("w_hi"), sem("w_lo"), sem("w_bias"), sem("c_b1")
        names = ("x_mv x_eps x_rstd qn_ready qT_psum qT_ready kT_psum kT_ready gate_psum gate_ready "
                 "absf e_ready log1p_ready lf_ready cs_psum a_ready lfsum_ready aT_psum at_ready ats_ready "
                 "ahi_ready an_psum an_ready abc_psum argA argB masked d_ready ex_ready fac_ready kg_ready qp_ready "
                 "qpT_psum qpT_ready score_psum pA pB h_psum nrm_a nrm_b nrm_c rec_ready h_ready upd_psum st_a "
                 "state_ready h_mv h_eps h_rstd hs_ready x1_ready o_mv o_eps o_rstd v_a o_eps2 "
                 "o_rstd3 u_ready r_a r_ready hn_ready hT_psum hT_ready").split()
        s = {n: sem(n) for n in names}
        fc1_done, pre_ready, y_ready, yhi_ready, ylo_ready, fc2_done = (
            sem(n) for n in ("fc1_done", "pre_ready", "y_ready", "yhi_ready", "ylo_ready", "fc2_done"))
        hhi_ready, hlo_ready, z_free = sem("hhi_ready"), sem("hlo_ready"), sem("z_free")

        block = es.enter_context(nc.Block())

        def wait(eng, semaphore, value):
            if not isinstance(value, int) or value > 0:
                eng.wait_ge(semaphore, value)

        def count7(b, c):
            return (CB - 1) * (b + c // CB) + min(c % CB + 1, CB - 1)

        def chunk_in(b, c):
            return not isinstance(b, int) or 0 <= CB * b + c < NG

        def unit_in(b, u):
            return not isinstance(b, int) or 0 <= UB * b + u < NU

        def slots(eng, slot):
            for c in range(CB - 1):
                slot(0, c)
            with eng.Fori(1, B) as b:
                for c in range(-1, CB - 1):
                    slot(b, c)
            for c in range(-1, LAG + 1):
                slot(B, c)

        def rows(eng, b, c):
            row = (CB * b + c) * P
            return bass.ds(row if isinstance(row, int) else eng.snap(row), P)

        def hv(t2d, e, w=DH):
            return t2d.rearrange("p (r e d) -> p r e d", e=2, d=w)[:, :, e, :]

        pieces = [(1, kt, nb) for nb in range(F // 512) for kt in range(KT)] + [(2, j, 0) for j in range(NJ)]
        PER = 8

        def piece_hi_lo(i):
            w, k, nb = pieces[i]
            cols = slice(nb * 512, nb * 512 + 512)
            return (w1h[:, k, cols], w1l[:, k, cols]) if w == 1 else (w2h[:, k, :], w2l[:, k, :])

        def pieces_at(b, c, sub):
            if isinstance(b, int) and b == 0 and c * PER + sub < len(pieces):
                yield c * PER + sub

        @block.sync
        def _(sp):
            for n, (wt, p0) in enumerate(((igate_w, 0), (fgate_w, NH))):
                for e in range(2):
                    sp.dma_start(gwraw[p0 + e * PR:p0 + e * PR + PR, :],
                                 wt.rearrange("(r e) k -> e r k", e=2)[e]).then_inc(l_gw, 16)
            for gb, c0 in ((igate_b, 0), (fgate_b, NH)):
                sp.dma_start(gbraw[:, c0:c0 + NH],
                             gb.rearrange("(o h) -> o h", o=1).broadcast_to([P, NH])).then_inc(l_const, 16)
            for g in range(2):
                sp.dma_start(xin[:, g, :], xf[rows(sp, 0, g), :]).then_inc(l_x[g], 16)
                sp.dma_start(vaug[:, g, :, 1:1 + P],
                             cf[rows(sp, 0, g), :].rearrange("p (r d) -> p r d", d=P)).then_inc(l_ctx[g], 16)
            sp.dma_start(lnsc[:, :], ln_scale.rearrange("(o d) -> o d", o=1).broadcast_to([P, D])).then_inc(l_const, 16)
            sp.dma_start(b2h[:, :], b2.rearrange("(o d) -> o d", o=1).broadcast_to([P, D])).then_inc(l_const, 16)
            sp.dma_start(gcol[:, :], gamma.rearrange("(k p) -> p k", p=P), allow_slow_non_contiguous=True).then_inc(l_bias, 16)
            sp.dma_start(bcol[:, :], beta.rearrange("(k p) -> p k", p=P), allow_slow_non_contiguous=True).then_inc(l_bias, 16)
            sp.dma_start(b1c[:, :], b1.rearrange("(k p) -> p k", p=P), allow_slow_non_contiguous=True).then_inc(l_bias, 16)

            def slot(b, c):
                g = CB * b + c
                if c % HC == 1 and unit_in(b, UPS * (c - LAG) - NJ):
                    n = g // HC - 2 if isinstance(b, int) else 2 * b + c // HC - 2
                    for m in range(HC):
                        dst = rows(sp, b, c + m - LAG - HC)
                        wait(sp, z_free, HC * n + m + 1)
                        sp.dma_start(of[dst, :], rin[:, m, :]).then_inc(rin_left[m], 16)
                for sub in range(PER):
                    for i in pieces_at(b, c, sub):
                        w, k, nb = pieces[i]
                        qd, sd, cols = (q1, s1, slice(nb * 512, nb * 512 + 512)) if w == 1 else (q2, s2, slice(0, 512))
                        wait(sp, w_raw, i - 1)
                        sp.dma_start(rin[:, i % 2, :].bitcast(I32), qd[k * P:(k + 1) * P, cols]).then_inc(l_q[i % 2], 16)
                        sp.dma_start(rin[:, 2 + i % 2, :], sd[k:k + 1, cols].broadcast_to([P, 512])).then_inc(l_s[i % 2], 16)
                    if sub == 2 and chunk_in(b, c + 1) and not (isinstance(b, int) and g == 0):
                        src = rows(sp, b, c + 1)
                        wait(sp, s["gate_psum"], g + 1)
                        sp.dma_start(vaug[:, (c + 1) % 2, :, 1:1 + P],
                                     cf[src, :].rearrange("p (r d) -> p r d", d=P)
                                     ).then_inc(l_ctx[(c + 1) % 2], 16)
                        wait(sp, s["x1_ready"], g)
                        sp.dma_start(xin[:, (c + 1) % 2, :], xf[src, :]).then_inc(l_x[(c + 1) % 2], 16)
                    if sub == 4 and chunk_in(b, c - 1):
                        dst = rows(sp, b, c - 1)
                        if c % HC == 0:
                            wait(sp, st_r, 16 * (g - HC))
                        wait(sp, s["r_ready"], g)
                        sp.dma_start(resid[dst, :], hx[:, :]).then_inc(st_r, 16)
                if c % HC == 0 and unit_in(b, UPS * (c + 1 - LAG) - NJ):
                    n = g // HC - 2 if isinstance(b, int) else 2 * b + c // HC - 2
                    for m in range(HC):
                        wait(sp, rin_left[m], 16 * (n + 1))
                        sp.dma_start(rin[:, m, :], resid[rows(sp, b, c + m - 2 * HC), :]).then_inc(l_rin[m], 16)

            slots(sp, slot)
            for m in range(HC):
                sp.wait_ge(rin_left[m], 16 * (NG // HC + 1))

        @block.gpsimd
        def _(pool):
            pool.memset(ident[:, :], 0.0).then_inc(c_zero, 1)
            pool.memset(tri[:, :], 1.0).then_inc(c_zero, 1)
            pool.memset(sel32[:, :], 0.0).then_inc(c_zero, 1)
            pool.memset(ones[:, :], 1.0).then_inc(c_ready, 1)
            pool.memset(neghalf[:, :], -0.5).then_inc(c_ready, 1)
            pool.memset(minit[:, :], NEG).then_inc(c_ready, 1)
            pool.memset(vaug[:, :, :, 0:1], 1.0).then_inc(c_ready, 1)
            pool.memset(vaug[:, :, :, 1 + P:2 + P], 1.0).then_inc(c_ready, 1)
            pool.wait_ge(c_zero, 3)
            pool.affine_select(out=ident[:, :], in_=ident[:, :], compare_op=ALU.not_equal, fill=1.0, base=0,
                               pattern=[[-1, P]], channel_multiplier=1).then_inc(c_ident, 1)
            pool.affine_select(out=tri[:, :], in_=tri[:, :], compare_op=ALU.is_ge, fill=0.0, base=0,
                               pattern=[[1, P]], channel_multiplier=-1).then_inc(c_ready, 1)
            pool.affine_select(out=sel32[:, :], in_=sel32[:, :], compare_op=ALU.not_equal, fill=1.0, base=0,
                               pattern=[[-1, NH]], channel_multiplier=1).then_inc(c_sel, 1)
            pool.wait_ge(c_sel, 1)
            pool.affine_select(out=sel32[:, :], in_=sel32[:, :], compare_op=ALU.not_equal, fill=1.0, base=-32,
                               pattern=[[-1, NH]], channel_multiplier=1).then_inc(c_sel, 1)
            pool.wait_ge(c_ready, 6)

            def rsqrt(src, dst, ready, done, value):
                wait(pool, ready, value)
                pool.tensor_tensor(dst, src, neghalf[:, :], ALU.pow).then_inc(done, 1)

            rsqrt(xmv[:, 2:3], xmv[:, 3:4], s["x_eps"], s["x_rstd"], 1)
            negfill = pool.to_reg(NEG)

            def slot(b, c):
                g = CB * b + c
                for sub in range(8):
                    if sub == 2 and chunk_in(b, c - 1):
                        rsqrt(hmv[:, 2:3], hmv[:, 3:4], s["h_eps"], s["h_rstd"], g)
                    if sub == 3 and chunk_in(b, c - 1):
                        rsqrt(omv[:, 2:3], omv[:, 3:4], s["o_eps"], s["o_rstd"], g)
                        rsqrt(omv[:, 5:6], omv[:, 6:7], s["o_eps2"], s["o_rstd3"], g)
                    if sub == 4 and chunk_in(b, c - 1):
                        wait(pool, s["u_ready"], g)
                        pool.tensor_tensor(hx[:, :], hx[:, :], kg_u[:, :], ALU.add).then_inc(s["r_a"], 1)
                        wait(pool, s["r_a"], g)
                        pool.tensor_tensor(hx[:, :], hx[:, :], b2h[:, :], ALU.add).then_inc(s["r_ready"], 1)
                    if sub == 5 and chunk_in(b, c + 1):
                        rsqrt(xmv[:, 2:3], xmv[:, 3:4], s["x_eps"], s["x_rstd"], g + 2)
                    if sub == 7 and chunk_in(b, c):
                        wait(pool, s["fac_ready"], g + 1)
                        wait(pool, s["qT_psum"], g + 1)
                        for e in range(2):
                            last = pool.tensor_tensor(
                                hv(qn[:, :], e), hv(qn[:, :], e),
                                fac[:, 0, e * PR:(e + 1) * PR].unsqueeze(2).broadcast_to([P, PR, DH]), ALU.mult)
                        last.then_inc(s["qp_ready"], 1)
                        dm = dmat[:, :, :, :].rearrange("p e r t -> p (e r) t")
                        pool.affine_select(out=dm, in_=dm, compare_op=ALU.is_ge, fill=negfill, base=0,
                                           pattern=[[0, NH], [1, P]], channel_multiplier=-1
                                           ).then_inc(s["masked"], 1)
                        if c % CB != CB - 1:
                            wait(pool, s["hT_psum"], g)
                            for e in range(2):
                                last = pool.tensor_tensor(
                                    hv(kg_u[:, :], e), vaug[:, c % 2, :, 1 + e * DH:1 + e * DH + DH],
                                    fac[:, 1, e * PR:(e + 1) * PR].unsqueeze(2).broadcast_to([P, PR, DH]), ALU.mult)
                            last.then_inc(s["kg_ready"], 1)

            slots(pool, slot)

        @block.scalar
        def _(act):
            act.wait_ge(c_gwT, 1)
            act.activation(wg[:, 0:KT, :].rearrange("p k h -> p (k h)"), bankA[:, 0:KT * 2 * NH], ACT.Copy,
                           scale=8.0).then_inc(c_gcopy, 1)
            act.activation(wg[:, KT:2 * KT, :].rearrange("p k h -> p (k h)"),
                           bankA[:, KT * 2 * NH:2 * KT * 2 * NH], ACT.Copy).then_inc(c_gcopy, 1)

            def slot(b, c):
                g = CB * b + c
                for sub in range(8):
                    u = UPS * (c - LAG) + sub // 2
                    if sub % 2 == 0 and unit_in(b, u):
                        U, j = UB * b + u, u % NJ
                        wait(act, fc1_done, U + 1)
                        wait(act, ylo_ready, U - 1)
                        act.activation(ybuf[:, u % 2, :], ypsum[u % 2][:, :], ACT.Identity, bias=b1c[:, j:j + 1])
                        wait(act, y_ready, U)
                        act.activation(tbuf[:, :], ypsum[u % 2][:, :], ACT.Tanh, bias=b1h[:, j:j + 1],
                                       scale=0.5).then_inc(pre_ready, 1)
                    if sub % 2 == 1 and unit_in(b, u):
                        U = UB * b + u
                        wait(act, fc2_done, U - 1)
                        wait(act, y_ready, U + 1)
                        act.activation(yhi[:, u % 2, :], ybuf[:, u % 2, :], ACT.Copy).then_inc(yhi_ready, 1)
                    for i in pieces_at(b, c, sub):
                        w, k, nb = pieces[i]
                        wait(act, w_raw, i + 1)
                        if i == 0:
                            act.wait_ge(l_bias, 48)
                        if w == 1:
                            act.activation(piece_hi_lo(i)[0], ybuf[:, i % 2, :], ACT.Copy,
                                           scale=gcol[:, k:k + 1]).then_inc(w_hi, 1)
                        else:
                            act.activation(piece_hi_lo(i)[0], ybuf[:, i % 2, :], ACT.Copy).then_inc(w_hi, 1)
                    if sub == 0 and chunk_in(b, c):
                        wait(act, s["qT_psum"], g + 1)
                        act.activation(qT[:, :, :].rearrange("p r t -> p (r t)"), bankA[:, :], ACT.Copy
                                       ).then_inc(s["qT_ready"], 1)
                        wait(act, s["kT_psum"], g + 1)
                        act.activation(kT[:, :, :].rearrange("p r t -> p (r t)"), bankB[:, :], ACT.Copy
                                       ).then_inc(s["kT_ready"], 1)
                    if sub == 3 and chunk_in(b, c):
                        wait(act, s["absf"], g + 1)
                        act.activation(gtmp[:, 1, :], gtmp[:, 0, :], ACT.Exp, scale=-1.0).then_inc(s["e_ready"], 1)
                        wait(act, s["e_ready"], g + 1)
                        act.activation(gtmp[:, 2, :], gtmp[:, 1, :], ACT.Ln, bias=1.0).then_inc(s["log1p_ready"], 1)
                    if sub == 4 and chunk_in(b, c - 1):
                        wait(act, s["r_a"], g)
                        wait(act, s["o_rstd3"], g)
                        act.activation(kg_u[:, :], kg_u[:, :], ACT.Copy, scale=omv[:, 6:7]).then_inc(s["hn_ready"], 1)
                    if sub == 5 and chunk_in(b, c - 1):
                        k = (c - 1) % HC
                        n = 2 * b + (c - 1) // HC
                        wait(act, s["hT_psum"], g)
                        wait(act, hlo_ready, KT * n)
                        act.activation(hstage[:, :, k * P:(k + 1) * P],
                                       bankA[:, :].rearrange("p (k t) -> p k t", t=P), ACT.Copy
                                       ).then_inc(s["hT_ready"], 1)
                    if sub == 7 and chunk_in(b, c):
                        wait(act, s["ex_ready"], g + 1)
                        wait(act, s["qp_ready"], g)
                        wait(act, s["kg_ready"], count7(b, c - 1))
                        act.activation(fac[:, :, :], ex[:, :, :], ACT.Exp).then_inc(s["fac_ready"], 1)
                        wait(act, s["masked"], g + 1)
                        act.activation(dmat[:, :, :, :], dmat[:, :, :, :], ACT.Exp).then_inc(s["d_ready"], 1)
                        wait(act, s["qpT_psum"], g + 1)
                        act.activation(qpT[:, :, :].rearrange("p r t -> p (r t)"), bankA[:, :], ACT.Copy
                                       ).then_inc(s["qpT_ready"], 1)
                    if sub == 7 and c % HC == 0 and unit_in(b, UPS * (c + 1 - LAG)):
                        n = 2 * b + c // HC - 1
                        wait(act, s["hT_ready"], HC * (n + 1))
                        wait(act, fc1_done, NJ * n)
                        for k in range(KT):
                            act.activation(hhi[:, k, :], hstage[:, k, :], ACT.Copy).then_inc(hhi_ready, 1)

            slots(act, slot)

        @block.vector
        def _(dve):
            def mean_var(src, st, mv, mvs, eps, value, scale=1.0):
                dve.bn_stats(st[:, :], src)
                dve.drain()
                dve.bn_aggr(mv[:, 0:2], st[:, :]).then_inc(mvs, 1)
                wait(dve, mvs, value)
                dve.tensor_scalar(mv[:, 2:3], mv[:, 1:2], LN_EPS, scale, ALU.add, ALU.mult).then_inc(eps, 1)

            def x_stats(b, c):
                g = CB * b + c
                wait(dve, l_x[c % 2], 16 * (4 * b + c // 2 + 1))
                mean_var(xin[:, c % 2, :], xst, xmv, s["x_mv"], s["x_eps"], g + 1, float(DH))

            def q_norm(b, c):
                g = CB * b + c
                wait(dve, s["x_rstd"], g + 1)
                wait(dve, s["qpT_psum"], g)
                dve.tensor_scalar(qn[:, :], xin[:, c % 2, :], xmv[:, 0:1], xmv[:, 3:4], ALU.subtract, ALU.mult
                                  ).then_inc(s["qn_ready"], 1)

            dve.memset(ats[:, :].bitcast(F32), 0.0).then_inc(c_dve, 1)
            x_stats(0, 0)
            dve.wait_ge(c_sel, 2)
            dve.tensor_copy(sel[:, :], sel32[:, :]).then_inc(c_dve, 1)
            dve.wait_ge(l_const, 64)
            for e in range(2):
                dve.tensor_copy(gbias[:, :].rearrange("p (g e r) -> p g e r", g=2, e=2)[:, :, e, :],
                                gbraw[:, :].rearrange("p (g r e) -> p g r e", g=2, e=2)[:, :, :, e]).then_inc(c_dve, 1)
            dve.tensor_scalar(b2h[:, :], b2h[:, :], 0.5, None, ALU.mult).then_inc(c_dve, 1)
            dve.wait_ge(c_gcopy, 2)
            dve.tensor_tensor(wg[:, KT:2 * KT, :].rearrange("p k h -> p (k h)"),
                              wg[:, KT:2 * KT, :].rearrange("p k h -> p (k h)"),
                              bankA[:, 2 * KT * 2 * NH:3 * KT * 2 * NH], ALU.add).then_inc(c_wg, 1)
            q_norm(0, 0)

            def slot(b, c):
                g = CB * b + c
                first = c % CB == 0
                for sub in range(8):
                    u = UPS * (c - LAG) + sub // 2
                    if sub % 2 == 0 and unit_in(b, u):
                        U = UB * b + u
                        wait(dve, pre_ready, U + 1)
                        dve.scalar_tensor_tensor(out=ybuf[:, u % 2, :], in0=tbuf[:, :], scalar=1.0,
                                                 in1=ybuf[:, u % 2, :], op0=ALU.add, op1=ALU.mult
                                                 ).then_inc(y_ready, 1)
                    for i in pieces_at(b, c, sub):
                        w, k, nb = pieces[i]
                        wait(dve, l_q[i % 2], 16 * (i // 2 + 1))
                        wait(dve, l_s[i % 2], 16 * (i // 2 + 1))
                        wait(dve, w_hi, i - 1)
                        wait(dve, w_bias, min(i - 1, 16))
                        dve.scalar_tensor_tensor(out=ybuf[:, i % 2, :], in0=rin[:, i % 2, :].bitcast(I32),
                                                 scalar=-128.0, in1=rin[:, 2 + i % 2, :], op0=ALU.add,
                                                 op1=ALU.mult).then_inc(w_raw, 1)
                        wait(dve, w_hi, i + 1)
                        hi, lo = piece_hi_lo(i)
                        if w == 1:
                            dve.scalar_tensor_tensor(out=lo, in0=ybuf[:, i % 2, :], scalar=gcol[:, k:k + 1],
                                                     in1=hi.bitcast(F32), op0=ALU.mult, op1=ALU.subtract
                                                     ).then_inc(w_lo, 1)
                        else:
                            dve.tensor_tensor(lo, ybuf[:, i % 2, :], hi.bitcast(F32), ALU.subtract
                                              ).then_inc(w_lo, 1)
                        if i == len(pieces) - 1:
                            for m in range(HC):
                                dve.drain().then_inc(rin_left[m], 16)
                            dve.wait_ge(w_bias, 16)
                            dve.tensor_tensor(b1c[:, :], b1c[:, :], ypsum[0][:, 0:NJ], ALU.add).then_inc(c_b1, 1)
                            dve.wait_ge(c_b1, 1)
                            dve.tensor_scalar(b1h[:, :], b1c[:, :], 0.5, None, ALU.mult).then_inc(c_b1, 1)
                    if sub == 0 and chunk_in(b, c - 1):
                        wait(dve, s["d_ready"], g)
                        wait(dve, s["score_psum"], g)
                        for e, (bank, done) in enumerate(((bankA, s["pA"]), (bankB, s["pB"]))):
                            dv = dmat[:, e, :, :].rearrange("p r t -> p (r t)")
                            dve.tensor_tensor(dv, dv, bank[:, :], ALU.mult).then_inc(done, 1)
                    if sub % 2 == 1 and unit_in(b, u):
                        U = UB * b + u
                        wait(dve, yhi_ready, U + 1)
                        dve.tensor_tensor(ylo[:, u % 2, :], ybuf[:, u % 2, :], yhi[:, u % 2, :].bitcast(F32),
                                          ALU.subtract).then_inc(ylo_ready, 1)
                    if sub == 1 and c % HC == 1 and unit_in(b, UPS * (c - LAG) - NJ):
                        n = 2 * b + c // HC - 2
                        for m in range(HC):
                            wait(dve, l_rin[m], 16 * (n + 1))
                            wait(dve, fc2_done, NJ * (n + 1))
                            dve.scalar_tensor_tensor(out=rin[:, m, :], in0=zpsum[m][:, :], scalar=0.25,
                                                     in1=rin[:, m, :], op0=ALU.mult, op1=ALU.add
                                                     ).then_inc(z_free, 1)
                    if sub == 1 and chunk_in(b, c - 1):
                        wait(dve, s["h_psum"], g)
                        wait(dve, s["fac_ready"], g)
                        sums = [bank[:, 0:PR * VW].rearrange("p (r w) -> p r w", w=VW)[:, :, e * DH]
                                for e, bank in enumerate((bankA, bankB))]
                        heads = [slice(e * PR, e * PR + PR) for e in range(2)]
                        for e in range(2):
                            last = dve.scalar_tensor_tensor(out=nrm[:, 0, heads[e]], in0=sums[e], scalar=-1.0,
                                                            in1=fac[:, 3, heads[e]], op0=ALU.mult, op1=ALU.max)
                        last.then_inc(s["nrm_a"], 1)
                        wait(dve, s["nrm_a"], g)
                        for e in range(2):
                            last = dve.tensor_tensor(nrm[:, 0, heads[e]], nrm[:, 0, heads[e]], sums[e], ALU.max)
                        last.then_inc(s["nrm_b"], 1)
                        wait(dve, s["nrm_b"], g)
                        dve.tensor_scalar(nrm[:, 0, :], nrm[:, 0, :], NORM_EPS, None, ALU.add).then_inc(s["nrm_c"], 1)
                        wait(dve, s["nrm_c"], g)
                        dve.reciprocal(nrm[:, 1, :], nrm[:, 0, :]).then_inc(s["rec_ready"], 1)
                        wait(dve, s["rec_ready"], g)
                        wait(dve, st_r, 16 * (g - 1))
                        for e, bank in enumerate((bankA, bankB)):
                            last = dve.tensor_tensor(
                                hv(hx[:, :], e), bank[:, 0:PR * VW].rearrange("p (r w) -> p r w", w=VW)[:, :, 1 - e:1 - e + DH],
                                nrm[:, 1, e * PR:e * PR + PR].unsqueeze(2).broadcast_to([P, PR, DH]), ALU.mult)
                        last.then_inc(s["h_ready"], 1)
                        wait(dve, s["h_ready"], g)
                        mean_var(hx[:, :], hst, hmv, s["h_mv"], s["h_eps"], g)
                    if sub == 2 and chunk_in(b, c - 1):
                        dve.scalar_tensor_tensor(out=hx[:, :], in0=hx[:, :], scalar=hmv[:, 0:1], in1=lnsc[:, :],
                                                 op0=ALU.subtract, op1=ALU.mult).then_inc(s["hs_ready"], 1)
                        wait(dve, s["hs_ready"], g)
                        wait(dve, s["h_rstd"], g)
                        dve.scalar_tensor_tensor(out=hx[:, :], in0=hx[:, :], scalar=hmv[:, 3:4],
                                                 in1=xin[:, (c - 1) % 2, :], op0=ALU.mult, op1=ALU.add
                                                 ).then_inc(s["x1_ready"], 1)
                        wait(dve, s["x1_ready"], g)
                        mean_var(hx[:, :], ost, omv, s["o_mv"], s["o_eps"], g)
                    if sub == 2 and chunk_in(b, c):
                        wait(dve, s["gate_psum"], g + 1)
                        dve.tensor_tensor(gate[:, :], bankA[:, 0:2 * NH], gbias[:, :], ALU.add
                                          ).then_inc(s["gate_ready"], 1)
                        wait(dve, s["gate_ready"], g + 1)
                        dve.scalar_tensor_tensor(out=gtmp[:, 0, :], in0=gate[:, NH:2 * NH], scalar=-1.0,
                                                 in1=gate[:, NH:2 * NH], op0=ALU.mult, op1=ALU.max
                                                 ).then_inc(s["absf"], 1)
                    if sub == 2 and chunk_in(b, c - 1):
                        if c % CB != 0:
                            if (c - 1) % CB == 0:
                                wait(dve, s["upd_psum"], count7(b, c - 1))
                                dve.tensor_copy(state[:, :, :].rearrange("p r w -> p (r w)"),
                                                bankB[:, 0:PR * VW]).then_inc(s["state_ready"], 1)
                            else:
                                for e in range(2):
                                    ps = slice(e * DH, e * DH + DH)
                                    last = dve.tensor_tensor(
                                        state[ps, :, :], state[ps, :, :],
                                        fac[ps, 2, e * PR:e * PR + PR].unsqueeze(2).broadcast_to([DH, PR, VW]),
                                        ALU.mult)
                                last.then_inc(s["st_a"], 1)
                                wait(dve, s["st_a"], (CB - 2) * (b + (c - 1) // CB) + (c - 1) % CB)
                                wait(dve, s["upd_psum"], count7(b, c - 1))
                                sf = state[:, :, :].rearrange("p r w -> p (r w)")
                                dve.tensor_tensor(sf, sf, bankB[:, 0:PR * VW], ALU.add
                                                  ).then_inc(s["state_ready"], 1)
                        wait(dve, s["o_rstd"], g)
                        dve.tensor_scalar(omv[:, 4:5], omv[:, 1:2], omv[:, 3:4], omv[:, 3:4], ALU.mult, ALU.mult
                                          ).then_inc(s["v_a"], 1)
                        wait(dve, s["v_a"], g)
                        dve.tensor_scalar(omv[:, 5:6], omv[:, 4:5], LN_EPS, None, ALU.add).then_inc(s["o_eps2"], 1)
                    if sub == 3 and chunk_in(b, c - 1):
                        if c % CB != 0:
                            wait(dve, s["upd_psum"], count7(b, c - 1))
                        dve.tensor_scalar(kg_u[:, :], hx[:, :], omv[:, 0:1], omv[:, 3:4], ALU.subtract, ALU.mult
                                          ).then_inc(s["u_ready"], 1)
                    if sub == 3 and chunk_in(b, c):
                        wait(dve, s["log1p_ready"], g + 1)
                        dve.scalar_tensor_tensor(out=lf[:, :], in0=gate[:, NH:2 * NH], scalar=0.0, in1=gtmp[:, 2, :],
                                                 op0=ALU.min, op1=ALU.subtract).then_inc(s["lf_ready"], 1)
                    if sub == 4 and chunk_in(b, c + 1):
                        x_stats(b, c + 1)
                    if sub == 4 and chunk_in(b, c):
                        wait(dve, s["cs_psum"], g + 1)
                        dve.tensor_copy(cs[:, :], bankA[:, 0:NH])
                        dve.tensor_tensor(acol[:, :], gate[:, 0:NH], bankA[:, 0:NH], ALU.subtract
                                          ).then_inc(s["a_ready"], 1)
                        if first:
                            dve.tensor_copy(lfsum[:, :], lf[:, :]).then_inc(s["lfsum_ready"], 1)
                        else:
                            dve.tensor_tensor(lfsum[:, :], lfsum[:, :], lf[:, :], ALU.add
                                              ).then_inc(s["lfsum_ready"], 1)
                    if sub == 5 and chunk_in(b, c):
                        wait(dve, s["aT_psum"], g + 1)
                        init = NEG if first else at[:, (c + 1) % 2, P - 1:P]
                        dve.tensor_tensor_scan(at[:, c % 2, :], bankB[0:NH, 0:P], minit[0:NH, 0:1].broadcast_to([NH, P]), init, ALU.max,
                                               ALU.max).then_inc(s["at_ready"], 1)
                        wait(dve, s["at_ready"], g + 1)
                        dve.tensor_copy(ats[0:NH, :], at[:, c % 2, :]).then_inc(s["ahi_ready"], 1)
                        wait(dve, s["ahi_ready"], g + 1)
                        dve.tensor_tensor(ats[32:32 + NH, :], at[:, c % 2, :], ats[0:NH, :].bitcast(F32),
                                          ALU.subtract).then_inc(s["ats_ready"], 1)
                    if sub == 6 and chunk_in(b, c):
                        wait(dve, s["an_psum"], g + 1)
                        dve.tensor_copy(an[:, :], bankA[:, 0:NH]).then_inc(s["an_ready"], 1)
                        wait(dve, s["abc_psum"], g + 1)
                        for e, (bank, done) in enumerate(((bankA, s["argA"]), (bankB, s["argB"]))):
                            bv = bank[:, :].rearrange("p (r t) -> p r t", t=P)
                            hs = slice(e * PR, e * PR + PR)
                            dve.tensor_copy(mnew[:, c % 2, hs], bv[:, :, P - 1])
                            dve.tensor_tensor(dmat[:, e, :, :], acol[:, hs].unsqueeze(2).broadcast_to([P, PR, P]),
                                              bv, ALU.subtract).then_inc(done, 1)
                        mprev = minit[:, :] if first else mnew[:, (c + 1) % 2, :]
                        wait(dve, s["argB"], g + 1)
                        wait(dve, s["an_ready"], g + 1)
                        dve.tensor_tensor(ex[:, 0, :], mprev, an[:, :], ALU.subtract)
                        dve.tensor_tensor(ex[:, 1, :], acol[:, :], mnew[:, c % 2, :], ALU.subtract)
                        dve.tensor_tensor(ex[:, 2, :], mprev, mnew[:, c % 2, :], ALU.subtract)
                        dve.scalar_tensor_tensor(out=ex[:, 3, :], in0=cs[:, :], scalar=-1.0, in1=an[:, :],
                                                 op0=ALU.mult, op1=ALU.subtract).then_inc(s["ex_ready"], 1)
                    if sub == 7 and c % HC == 0 and unit_in(b, UPS * (c + 1 - LAG)):
                        n = 2 * b + c // HC - 1
                        for k in range(KT):
                            wait(dve, hhi_ready, KT * n + k + 1)
                            dve.tensor_tensor(hlo[:, k, :], hstage[:, k, :], hhi[:, k, :].bitcast(F32),
                                              ALU.subtract).then_inc(hlo_ready, 1)
                    if sub == 7 and chunk_in(b, c + 1):
                        q_norm(b, c + 1)

            slots(dve, slot)

        @block.tensor
        def _(pe):
            pe.wait_ge(c_ident, 1)
            pe.wait_ge(l_gw, 64)
            for k in range(3 * KT):
                last = pe.transpose(bankA[:, k * 2 * NH:(k + 1) * 2 * NH], gwraw[:, k * P:(k + 1) * P],
                                    ident[0:2 * NH, 0:2 * NH])
            last.then_inc(c_gwT, 1)
            pe.wait_ge(c_ready, 6)
            pe.wait_ge(c_dve, 5)
            pe.wait_ge(c_wg, 1)

            def fc1(b, u):
                U, j = UB * b + u, u % NJ
                n = 2 * b + u // NJ
                wait(pe, pre_ready, U - 1)
                if isinstance(U, int) and U == 0:
                    pe.wait_ge(w_lo, len(pieces))
                    pe.wait_ge(c_b1, 2)
                cols = slice(j * P, (j + 1) * P)
                terms = ((w1h, hhi, hhi_ready), (w1l, hhi, None), (w1h, hlo, hlo_ready))
                for t, (wt, ht, ready) in enumerate(terms):
                    for k in range(KT):
                        if j == 0 and ready is not None:
                            wait(pe, ready, KT * n + k + 1)
                        last = pe.matmul(ypsum[u % 2][:, :], wt[:, k, cols], ht[:, k, :],
                                         start=(t == 0 and k == 0), stop=(t == 2 and k == KT - 1))
                last.then_inc(fc1_done, 1)

            def fc2(b, u):
                U, j = UB * b + u, u % NJ
                n = 2 * b + u // NJ
                wait(pe, yhi_ready, U + 1)
                wait(pe, ylo_ready, U + 1)
                for m in range(HC):
                    if j == 0:
                        wait(pe, z_free, HC * (n - 1) + m + 1)
                    ms = slice(m * P, (m + 1) * P)
                    for t, (yt, wt) in enumerate(((yhi, w2h), (yhi, w2l), (ylo, w2h))):
                        last = pe.matmul(zpsum[m][:, :], yt[:, u % 2, ms], wt[:, j, :],
                                         start=(j == 0 and t == 0), stop=(j == NJ - 1 and t == 2))
                last.then_inc(fc2_done, 1)

            def slot(b, c):
                g = CB * b + c
                front, back = chunk_in(b, c), chunk_in(b, c - 1)
                for sub in range(8):
                    u = UPS * (c - LAG) + sub // 2
                    if sub % 2 == 0 and unit_in(b, u):
                        fc1(b, u)
                    if sub % 2 == 1 and unit_in(b, u - 1):
                        fc2(b, u - 1)
                    for i in pieces_at(b, c, sub):
                        if pieces[i][0] == 1:
                            _, k, nb = pieces[i]
                            pe.wait_ge(w_raw, i + 1)
                            pe.wait_ge(l_bias, 48)
                            for jj in range(512 // P):
                                j = nb * (512 // P) + jj
                                last = pe.matmul(ypsum[0][:, j:j + 1], ybuf[:, i % 2, jj * P:(jj + 1) * P],
                                                 bcol[:, k:k + 1], start=(i == 0 and jj == 0), stop=False,
                                                 skip_group_check=True)
                            last.then_inc(w_bias, 1)
                    if sub == 0 and front:
                        wait(pe, s["qn_ready"], g + 1)
                        wait(pe, s["pA"], g)
                        for k in range(KT):
                            last = pe.transpose(bankA[:, k * P:(k + 1) * P], qn[:, k * P:(k + 1) * P], ident[:, :])
                        last.then_inc(s["qT_psum"], 1)
                        wait(pe, l_ctx[c % 2], 16 * (4 * b + c // 2 + 1))
                        wait(pe, s["pB"], g)
                        for k in range(KT):
                            last = pe.transpose(bankB[:, k * P:(k + 1) * P], vaug[:, c % 2, k, 1:1 + P],
                                                ident[:, :])
                        last.then_inc(s["kT_psum"], 1)
                    if sub == 1 and back:
                        wait(pe, s["pA"], g)
                        wait(pe, s["pB"], g)
                        if front:
                            wait(pe, s["qT_ready"], g + 1)
                            wait(pe, s["kT_ready"], g + 1)
                        inter = (c - 1) % CB != 0
                        if inter:
                            wait(pe, s["state_ready"], count7(b, c - 2))
                        for pr in range(PR):
                            for e, bank in enumerate((bankA, bankB)):
                                o = bank[:, pr * VW:(pr + 1) * VW]
                                last = pe.matmul(o, dmat[:, e, pr, :], vaug[:, (c - 1) % 2, pr, e * VW:(e + 1) * VW],
                                                 start=True, stop=not inter)
                                if inter:
                                    ps = slice(e * DH, e * DH + DH)
                                    last = pe.matmul(o, qpT[ps, pr, :], state[ps, pr, :], start=False, stop=True)
                        last.then_inc(s["h_psum"], 1)
                    if sub == 2 and back and c % CB != 0:
                        wait(pe, s["h_ready"], g)
                        wait(pe, s["kg_ready"], count7(b, c - 1))
                        for pr in range(PR):
                            for e in range(2):
                                h0 = (2 * pr + e) * DH
                                last = pe.matmul(bankB[e * DH:e * DH + DH, pr * VW:(pr + 1) * VW],
                                                 kg_u[:, h0:h0 + DH], vaug[:, (c - 1) % 2, pr, e * VW:(e + 1) * VW],
                                                 start=True, stop=True)
                        last.then_inc(s["upd_psum"], 1)
                    if sub == 2 and front:
                        wait(pe, s["h_ready"], g)
                        wait(pe, s["qT_ready"], g + 1)
                        wait(pe, s["kT_ready"], g + 1)
                        for k in range(2 * KT):
                            src = qT[:, k, :] if k < KT else kT[:, k - KT, :]
                            last = pe.matmul(bankA[:, 0:2 * NH], src, wg[:, k, :], start=(k == 0),
                                             stop=(k == 2 * KT - 1))
                        last.then_inc(s["gate_psum"], 1)
                    if sub == 4 and front:
                        wait(pe, s["gate_ready"], g + 1)
                        wait(pe, s["lf_ready"], g + 1)
                        last = pe.matmul(bankA[:, 0:NH], tri[:, :], lf[:, :], start=True, stop=c % CB == 0)
                        if c % CB != 0:
                            wait(pe, s["lfsum_ready"], g)
                            last = pe.matmul(bankA[:, 0:NH], ones[:, 0:1].broadcast_to([P, P]), lfsum[:, :], start=False, stop=True)
                        last.then_inc(s["cs_psum"], 1)
                    if sub == 5 and front:
                        wait(pe, s["a_ready"], g + 1)
                        if c % CB != 0:
                            wait(pe, s["state_ready"], count7(b, c - 1))
                        pe.transpose(bankB[0:NH, 0:P], acol[:, :], ident[:, :]).then_inc(s["aT_psum"], 1)
                    if sub == 5 and back:
                        wait(pe, s["hn_ready"], g)
                        if front:
                            wait(pe, s["a_ready"], g + 1)
                        for k in range(KT):
                            last = pe.transpose(bankA[:, k * P:(k + 1) * P], kg_u[:, k * P:(k + 1) * P], ident[:, :])
                        last.then_inc(s["hT_psum"], 1)
                    if sub == 6 and front:
                        wait(pe, s["hT_ready"], g)
                        wait(pe, s["ats_ready"], g + 1)
                        for e, bank in ((1, bankB), (0, bankA)):
                            if e == 0:
                                pe.transpose(bankA[:, 0:NH], at[:, c % 2, :], ident[0:NH, 0:NH]
                                             ).then_inc(s["an_psum"], 1)
                                wait(pe, s["an_ready"], g + 1)
                            for pr in range(PR):
                                h = e * PR + pr
                                last = pe.matmul(bank[:, pr * P:(pr + 1) * P],
                                                 sel[:, h:h + 1].broadcast_to([40, P]), ats[:, :],
                                                 start=True, stop=True)
                        last.then_inc(s["abc_psum"], 1)
                    if sub == 7 and front:
                        wait(pe, s["qp_ready"], g + 1)
                        wait(pe, s["argA"], g + 1)
                        for k in range(KT):
                            last = pe.transpose(bankA[:, k * P:(k + 1) * P], qn[:, k * P:(k + 1) * P], ident[:, :])
                        last.then_inc(s["qpT_psum"], 1)
                        wait(pe, s["argB"], g + 1)
                        wait(pe, s["qpT_ready"], g + 1)
                        for pr in range(PR):
                            for e, bank in enumerate((bankA, bankB)):
                                ps = slice(e * DH, e * DH + DH)
                                last = pe.matmul(bank[:, pr * P:(pr + 1) * P], kT[ps, pr, :], qT[ps, pr, :],
                                                 start=True, stop=True)
                        last.then_inc(s["score_psum"], 1)

            slots(pe, slot)


_INS = ['x', 'ctx_1024', 'L0_xattn_igate_w', 'L0_xattn_igate_b', 'L0_xattn_fgate_w', 'L0_xattn_fgate_b',
        'L0_xattn_ln_scale', 'L0_ffn_ln_gamma', 'L0_ffn_ln_beta', 'L0_ffn_fc1_q', 'L0_ffn_fc1_scales',
        'L0_ffn_fc1_bias', 'L0_ffn_fc2_q', 'L0_ffn_fc2_scales', 'L0_ffn_fc2_bias']


def kernel(**inputs):
    import numpy as _np
    import concourse.bacc as _bacc
    from concourse import mybir as _mybir
    from concourse.bass_utils import run_bass_kernel_spmd as _run

    nc = _bacc.Bacc("TRN2", target_bir_lowering=False, num_devices=1)
    arrays, args = {}, []
    for name in _INS:
        a = _np.ascontiguousarray(inputs[name])
        arrays[f"in_{name}_dram"] = a
        args.append(nc.dram_tensor(f"in_{name}_dram", a.shape, _mybir.dt.from_np(a.dtype), kind="ExternalInput").ap())
    shape = tuple(inputs['x'].shape)
    args.append(nc.dram_tensor("out_0_dram", shape, F32, kind="ExternalOutput").ap())
    build(nc, *args)
    r = _run(nc, [arrays], core_ids=[0])
    return r.results[0]["out_0_dram"]
```

```python
from contextlib import ExitStack

import concourse.bass as bass
from concourse import mybir

P = 128
ALU = mybir.AluOpType
ACT = mybir.ActivationFunctionType
F32 = mybir.dt.float32
F32R = mybir.dt.float32r
I32 = mybir.dt.int32

LN_EPS = 1e-5
NORM_EPS = 1e-6
NEG = -1e30
ATANH = [0.33333130962, 0.20014333164, 0.13950958323, 0.14223834211]
LAG = 5


def build(nc, x, ctx, igate_w, igate_b, fgate_w, fgate_b, ln_scale, gamma, beta,
          q1, s1, b1, q2, s2, b2, out):
    B, S, D = x.shape
    NH = igate_w.shape[0]
    DH = D // NH
    PR = NH // 2
    KT = D // P
    F = q1.shape[1]
    NJ = F // P
    CB = S // P
    NG = B * CB
    HC = 4
    R = HC * P
    NU = NJ * NG // HC
    UB = NJ * CB // HC
    UPS = NJ // HC
    POS = 4 * UPS
    Z_POS = (9, 10, 11, 12)
    VW = DH + 1
    assert KT == PR and DH * 2 == P and UPS == 4

    xf = x.rearrange("b s d -> (b s) d")
    cf = ctx.rearrange("b s d -> (b s) d")
    of = out.rearrange("b s d -> (b s) d")
    resid = nc.dram_tensor("resid_scratch", [NG * P, D], F32, kind="Internal").ap()

    with ExitStack() as es:
        def sb(name, shape, dt=F32):
            return es.enter_context(nc.sbuf_tensor(name, shape, dt))

        def pb(name):
            return es.enter_context(nc.psum_tensor(name, [P, 512], F32))

        def sem(name):
            return es.enter_context(nc.semaphore(name))

        w1 = sb("w1", [P, KT, F], F32R)
        w2h = sb("w2h", [P, NJ, D], F32R)
        w2l = sb("w2l", [P, NJ, D], F32R)
        hstage = sb("hstage", [P, KT, P])
        hhi = sb("hhi", [P, 2, KT, R], F32R)
        hlo = sb("hlo", [P, 2, KT, R], F32R)
        ybuf = sb("ybuf", [P, 2, R])
        tbuf = sb("tbuf", [P, R])
        vhalf = sb("vhalf", [P, R])
        yhi = sb("yhi", [P, 4, R], F32R)
        ylo = sb("ylo", [P, 4, R], F32R)
        rin = sb("rin", [P, HC, D])
        xin = sb("xin", [P, 2, D])
        vaug = sb("vaug", [P, 2, PR, 2 * VW])
        qn = sb("qn", [P, D])
        kg = sb("kg", [P, D])
        hn = sb("hn", [P, D])
        qT = sb("qT", [P, PR, P])
        kT = sb("kT", [P, PR, P])
        hint = sb("hint", [P, PR, 2, VW])
        dmat = sb("dmat", [P, 2, PR, P])
        hx = sb("hx", [P, D])
        state = sb("state", [P, PR, 2, VW])
        ident = sb("ident", [P, P])
        tri = sb("tri", [P, P])
        ones = sb("ones", [P, 1])
        lnsc = sb("lnsc", [P, D])
        b2h = sb("b2h", [P, D])
        wg = sb("wg", [P, 2 * KT, 2 * NH])
        gbias = sb("gbias", [P, 2 * NH])
        gbraw = sb("gbraw", [P, 2 * NH])
        gcol = sb("gcol", [P, KT])
        bcol = sb("bcol", [P, KT])
        b1c = sb("b1c", [P, NJ])
        s1c = sb("s1c", [P, KT * NJ])
        neghalf = sb("neghalf", [P, 2])
        carry = sb("carry", [P, 1])
        minit = sb("minit", [P, NH])
        sel = sb("sel", [40, NH], F32R)
        sel32 = sb("sel32", [40, NH])
        at = sb("at", [NH, 2, P])
        ats = sb("ats", [40, P], F32R)
        xst = sb("xst", [P, 6])
        xmv = sb("xmv", [P, 4])
        hst = sb("hst", [P, 6])
        hmv = sb("hmv", [P, 4])
        ost = sb("ost", [P, 6])
        omv = sb("omv", [P, 8])
        gate = sb("gate", [P, 2 * NH])
        gtmp = sb("gtmp", [P, 2, NH])
        ser = sb("ser", [P, 4, NH])
        lf = sb("lf", [P, NH])
        lfsum = sb("lfsum", [P, NH])
        cs = sb("cs", [P, NH])
        acol = sb("acol", [P, NH])
        an = sb("an", [P, NH])
        mnew = sb("mnew", [P, 2, NH])
        ex = sb("ex", [P, 4, NH])
        fac = sb("fac", [P, 4, NH])
        nrm = sb("nrm", [P, 2, NH])
        gwraw = [t[0:2 * NH, :] for t in (tbuf, vhalf, hx)]
        s1raw = ybuf[0:KT * NJ, 0, 0:P]

        bankA, bankB = pb("bankA"), pb("bankB")
        ypsum = [pb("ypsum0"), pb("ypsum1")]
        zpsum = [pb(f"zpsum{m}") for m in range(HC)]

        l_const, l_gw, l_bias, l_s1c = sem("l_const"), sem("l_gw"), sem("l_bias"), sem("l_s1c")
        l_q1, l_q2, l_s2 = [sem("l_q1_0"), sem("l_q1_1")], sem("l_q2"), sem("l_s2")
        l_x = [sem("l_x0"), sem("l_x1")]
        l_ctx = [sem("l_ctx0"), sem("l_ctx1")]
        l_rin = [sem(f"l_rin{m}") for m in range(HC)]
        st_r = sem("st_r")
        rin_left = [sem(f"rin_left{m}") for m in range(HC)]
        c_zero, c_ident, c_gwT, c_ready = sem("c_zero"), sem("c_ident"), sem("c_gwT"), sem("c_ready")
        c_sel, c_gcopy, c_wg, c_dve = sem("c_sel"), sem("c_gcopy"), sem("c_wg"), sem("c_dve")
        w_one, w_raw, w_hi, w_lo = sem("w_one"), sem("w_raw"), sem("w_hi"), sem("w_lo")
        names = ("x_mv x_eps x_rstd qn_ready qT_psum qT_ready kT_psum kT_ready gate_psum gate_ready "
                 "absf e_ready lf_ready cs_psum a_ready lfsum_ready aT_psum at_ready ats_ready "
                 "ahi_ready an_psum an_ready abc_psum argA argB masked d_ready ex_ready fac_ready kg_ready "
                 "inter_psum hint_raw hint_ready score_psum pA pB h_psum sum_ready nrm_a nrm_b nrm_c rec_ready "
                 "h_evac h_ready upd_psum st_a state_ready h_mv h_eps h_rstd hs_ready x1_ready o_mv o_eps o_rstd r_coef "
                 "r_a r_ready hn_ready hT_psum hT_ready hg_ready").split()
        s = {n: sem(n) for n in names}
        fc1_part, part_act, part_dve, v_ready, pre_ready, y_ready, yhi_ready, ylo_ready, fc2_part = (
            sem(n) for n in ("fc1_part", "part_act", "part_dve", "v_ready", "pre_ready", "y_ready", "yhi_ready",
                             "ylo_ready", "fc2_part"))
        hhi_ready, hlo_ready, z_free = sem("hhi_ready"), sem("hlo_ready"), sem("z_free")

        block = es.enter_context(nc.Block())

        def wait(eng, semaphore, value):
            if not isinstance(value, int) or value > 0:
                eng.wait_ge(semaphore, value)

        def count7(b, c):
            return (CB - 1) * (b + c // CB) + min(c % CB + 1, CB - 1)

        def chunk_in(b, c):
            return not isinstance(b, int) or 0 <= CB * b + c < NG

        def unit_in(b, u):
            return not isinstance(b, int) or 0 <= UB * b + u < NU

        def slots(eng, slot):
            for c in range(CB - 1):
                slot(0, c)
            with eng.Fori(1, B) as b:
                for c in range(-1, CB - 1):
                    slot(b, c)
            for c in range(-1, LAG + 1):
                slot(B, c)

        def rows(eng, b, c):
            row = (CB * b + c) * P
            return bass.ds(row if isinstance(row, int) else eng.snap(row), P)

        def hv(t2d, e, w=DH):
            return t2d.rearrange("p (r e d) -> p r e d", e=2, d=w)[:, :, e, :]

        w1_pieces = [(kt, slice(nb * 512, nb * 512 + 512)) for nb in range(F // 512) for kt in range(KT)]
        assert len(w1_pieces) == NJ

        def piece_at(b, c, pos, first):
            i = (POS * c + pos - first) // 4
            return isinstance(b, int) and b == 0 and (pos - first) % 4 == 0 and 0 <= i < NJ, i

        @block.sync
        def _(sp):
            for n, (wt, p0) in enumerate(((igate_w, 0), (fgate_w, NH))):
                for e in range(2):
                    for part in range(3):
                        sp.dma_start(gwraw[part][p0 + e * PR:p0 + e * PR + PR, :],
                                     wt.rearrange("(r e) k -> e r k", e=2)[e][:, part * D:(part + 1) * D]
                                     ).then_inc(l_gw, 16)
            for gb, c0 in ((igate_b, 0), (fgate_b, NH)):
                sp.dma_start(gbraw[:, c0:c0 + NH],
                             gb.rearrange("(o h) -> o h", o=1).broadcast_to([P, NH])).then_inc(l_const, 16)
            sp.dma_start(s1raw, s1.rearrange("k (j p) -> (k j) p", p=P)).then_inc(l_s1c, 16)
            for g in range(2):
                sp.dma_start(xin[:, g, :], xf[rows(sp, 0, g), :]).then_inc(l_x[g], 16)
                sp.dma_start(vaug[:, g, :, 1:1 + P],
                             cf[rows(sp, 0, g), :].rearrange("p (r d) -> p r d", d=P)).then_inc(l_ctx[g], 16)
            sp.dma_start(lnsc[:, :], ln_scale.rearrange("(o d) -> o d", o=1).broadcast_to([P, D])).then_inc(l_const, 16)
            sp.dma_start(b2h[:, :], b2.rearrange("(o d) -> o d", o=1).broadcast_to([P, D])).then_inc(l_const, 16)
            sp.dma_start(gcol[:, :], gamma.rearrange("(k p) -> p k", p=P), allow_slow_non_contiguous=True).then_inc(l_bias, 16)
            sp.dma_start(bcol[:, :], beta.rearrange("(k p) -> p k", p=P), allow_slow_non_contiguous=True).then_inc(l_bias, 16)
            sp.dma_start(b1c[:, :], b1.rearrange("(k p) -> p k", p=P), allow_slow_non_contiguous=True).then_inc(l_bias, 16)

            def slot(b, c):
                g = CB * b + c
                for pos in range(POS):
                    due, i = piece_at(b, c, pos, 0)
                    if due:
                        k, cols = w1_pieces[i]
                        wait(sp, w_one, i - 1)
                        sp.dma_start(rin[:, i % 2, :].bitcast(I32), q1[k * P:(k + 1) * P, cols]).then_inc(l_q1[i % 2], 16)
                    due, i = piece_at(b, c, pos, 1)
                    if due:
                        wait(sp, w_raw, i)
                        sp.dma_start(rin[:, 2, :].bitcast(I32), q2[i * P:(i + 1) * P, :]).then_inc(l_q2, 16)
                        sp.dma_start(rin[:, 3, :], s2[i:i + 1, :].broadcast_to([P, D])).then_inc(l_s2, 16)
                    if pos == 6 and chunk_in(b, c + 1) and not (isinstance(b, int) and g == 0):
                        src = rows(sp, b, c + 1)
                        wait(sp, s["cs_psum"], g + 1)
                        sp.dma_start(vaug[:, (c + 1) % 2, :, 1:1 + P],
                                     cf[src, :].rearrange("p (r d) -> p r d", d=P)
                                     ).then_inc(l_ctx[(c + 1) % 2], 16)
                        wait(sp, s["x1_ready"], g)
                        sp.dma_start(xin[:, (c + 1) % 2, :], xf[src, :]).then_inc(l_x[(c + 1) % 2], 16)
                    if pos == 15 and chunk_in(b, c - 1):
                        dst = rows(sp, b, c - 1)
                        if c % HC == 0:
                            wait(sp, st_r, 16 * (g - HC))
                        wait(sp, s["r_ready"], g)
                        sp.dma_start(resid[dst, :], hx[:, :]).then_inc(st_r, 16)
                    if pos == 15 and c % HC == 1 and unit_in(b, UPS * (c - LAG) - NJ):
                        n = g // HC - 2 if isinstance(b, int) else 2 * b + c // HC - 2
                        for m in range(HC):
                            dst = rows(sp, b, c + m - LAG - HC)
                            wait(sp, z_free, HC * n + m + 1)
                            sp.dma_start(of[dst, :], rin[:, m, :]).then_inc(rin_left[m], 16)
                if c % HC == 0 and unit_in(b, UPS * (c + 1 - LAG) - NJ):
                    n = g // HC - 2 if isinstance(b, int) else 2 * b + c // HC - 2
                    for m in range(HC):
                        wait(sp, rin_left[m], 16 * (n + 1))
                        sp.dma_start(rin[:, m, :], resid[rows(sp, b, c + m - 2 * HC), :]).then_inc(l_rin[m], 16)

            slots(sp, slot)
            for m in range(HC):
                sp.wait_ge(rin_left[m], 16 * (NG // HC + 1))

        @block.gpsimd
        def _(pool):
            pool.memset(ident[:, :], 0.0).then_inc(c_zero, 1)
            pool.memset(tri[:, :], 1.0).then_inc(c_zero, 1)
            pool.memset(sel32[:, :], 0.0).then_inc(c_zero, 1)
            pool.memset(ones[:, :], 1.0).then_inc(c_ready, 1)
            pool.memset(neghalf[:, :], -0.5).then_inc(c_ready, 1)
            pool.memset(minit[:, :], NEG).then_inc(c_ready, 1)
            pool.memset(state[:, :, :, :], 0.0).then_inc(c_ready, 1)
            pool.memset(vaug[:, :, :, 0:1], 1.0).then_inc(c_ready, 1)
            pool.memset(vaug[:, :, :, 1 + P:2 + P], 1.0).then_inc(c_ready, 1)
            pool.wait_ge(c_zero, 3)
            pool.affine_select(out=ident[:, :], in_=ident[:, :], compare_op=ALU.not_equal, fill=1.0, base=0,
                               pattern=[[-1, P]], channel_multiplier=1).then_inc(c_ident, 1)
            pool.affine_select(out=tri[:, :], in_=tri[:, :], compare_op=ALU.is_ge, fill=0.0, base=0,
                               pattern=[[1, P]], channel_multiplier=-1).then_inc(c_ready, 1)
            pool.affine_select(out=sel32[:, :], in_=sel32[:, :], compare_op=ALU.not_equal, fill=1.0, base=0,
                               pattern=[[-1, NH]], channel_multiplier=1).then_inc(c_sel, 1)
            pool.wait_ge(c_sel, 1)
            pool.affine_select(out=sel32[:, :], in_=sel32[:, :], compare_op=ALU.not_equal, fill=1.0, base=-32,
                               pattern=[[-1, NH]], channel_multiplier=1).then_inc(c_sel, 1)
            pool.wait_ge(c_ready, 7)

            def rsqrt(src, dst, ready, done, value):
                wait(pool, ready, value)
                pool.tensor_tensor(dst, src, neghalf[:, 0:src.shape[-1]], ALU.pow).then_inc(done, 1)

            rsqrt(xmv[:, 2:3], xmv[:, 3:4], s["x_eps"], s["x_rstd"], 1)
            negfill = pool.to_reg(NEG)

            def slot(b, c):
                g = CB * b + c
                for pos in range(POS):
                    u = UPS * (c - LAG) + pos // 4
                    if pos == 7 and chunk_in(b, c - 1):
                        rsqrt(omv[:, 2:4], omv[:, 4:6], s["o_eps"], s["o_rstd"], g)
                    if pos % 4 == 3 and unit_in(b, u):
                        wait(pool, part_dve, 2 * (UB * b + u) + 2)
                        pool.tensor_tensor(ybuf[:, u % 2, :], ybuf[:, u % 2, :], vhalf[:, :], ALU.add
                                           ).then_inc(v_ready, 1)
                    if pos == 3 and chunk_in(b, c - 1):
                        rsqrt(hmv[:, 2:3], hmv[:, 3:4], s["h_eps"], s["h_rstd"], g)
                    if pos == 10 and chunk_in(b, c + 1):
                        rsqrt(xmv[:, 2:3], xmv[:, 3:4], s["x_eps"], s["x_rstd"], g + 2)
                    if pos == 0 and chunk_in(b, c - 1) and c % CB > 1:
                        st = state[:, :, :, :].rearrange("p r e w -> p r (e w)")
                        pool.tensor_tensor(st, st, fac[:, 2, 0:PR].unsqueeze(2).broadcast_to([P, PR, 2 * VW]), ALU.mult
                                           ).then_inc(s["st_a"], 1)
                    if pos == 2 and chunk_in(b, c - 1):
                        wait(pool, s["rec_ready"], g)
                        wait(pool, s["h_evac"], g)
                        for e in range(2):
                            last = pool.tensor_tensor(
                                hv(hx[:, :], e), hv(hx[:, :], e),
                                nrm[:, 1, e * PR:e * PR + PR].unsqueeze(2).broadcast_to([P, PR, DH]), ALU.mult)
                        last.then_inc(s["h_ready"], 1)
                    if pos % 4 == 2 and unit_in(b, u - 1):
                        wait(pool, yhi_ready, UB * b + u)
                        pool.tensor_tensor(ylo[:, (u - 1) % 4, :], ybuf[:, (u - 1) % 2, :],
                                          yhi[:, (u - 1) % 4, :].bitcast(F32), ALU.subtract).then_inc(ylo_ready, 1)
                    if pos == 12:
                        if chunk_in(b, c):
                            wait(pool, s["argA"], g + 1)
                            wait(pool, s["argB"], g + 1)
                            pool.tensor_tensor(carry[:, :], neghalf[:, 0:1], neghalf[:, 0:1], ALU.add)
                    if pos == 13 and chunk_in(b, c):
                        dm = dmat[:, :, :, :].rearrange("p e r t -> p (e r) t")
                        pool.affine_select(out=dm, in_=dm, compare_op=ALU.is_ge, fill=negfill, base=0,
                                           pattern=[[0, NH], [1, P]], channel_multiplier=-1
                                           ).then_inc(s["masked"], 1)
                        if c % CB == 0:
                            pool.memset(hint[:, :, :, :], 0.0).then_inc(s["hint_ready"], 1)
                        else:
                            wait(pool, s["hint_raw"], count7(b, c - 1))
                            wait(pool, s["fac_ready"], g + 1)
                            for e in range(2):
                                last = pool.tensor_tensor(
                                    hint[:, :, e, :], hint[:, :, e, :],
                                    fac[:, 0, e * PR:(e + 1) * PR].unsqueeze(2).broadcast_to([P, PR, VW]), ALU.mult)
                            last.then_inc(s["hint_ready"], 1)
                        if c % CB != CB - 1:
                            wait(pool, s["upd_psum"], count7(b, c - 1))
                            wait(pool, s["fac_ready"], g + 1)
                            for e in range(2):
                                last = pool.tensor_tensor(
                                    hv(kg[:, :], e), vaug[:, c % 2, :, 1 + e * DH:1 + e * DH + DH],
                                    fac[:, 1, e * PR:(e + 1) * PR].unsqueeze(2).broadcast_to([P, PR, DH]), ALU.mult)
                            last.then_inc(s["kg_ready"], 1)
                    if pos == 14:
                        if chunk_in(b, c - 1):
                            wait(pool, s["r_a"], g)
                            pool.tensor_tensor(hx[:, :], hx[:, :], b2h[:, :], ALU.add).then_inc(s["r_ready"], 1)

            slots(pool, slot)

        @block.scalar
        def _(act):
            act.wait_ge(c_gwT, 1)
            act.activation(wg[:, 0:KT, :].rearrange("p k h -> p (k h)"), bankA[:, 0:KT * 2 * NH], ACT.Copy,
                           scale=8.0).then_inc(c_gcopy, 1)
            act.activation(wg[:, KT:2 * KT, :].rearrange("p k h -> p (k h)"),
                           bankA[:, KT * 2 * NH:2 * KT * 2 * NH], ACT.Copy).then_inc(c_gcopy, 1)
            act.activation(s1c[:, :], bankB[:, 0:KT * NJ], ACT.Copy).then_inc(c_gcopy, 1)

            def slot(b, c):
                g = CB * b + c
                for pos in range(POS):
                    u = UPS * (c - LAG) + pos // 4
                    j = u % NJ
                    if pos % 4 == 0 and unit_in(b, u):
                        U = UB * b + u
                        wait(act, fc1_part, 4 * U + 1)
                        wait(act, ylo_ready, U - 1)
                        act.activation(ybuf[:, u % 2, :], ypsum[0][:, :], ACT.Identity, bias=b1c[:, j:j + 1],
                                       scale=s1c[:, j:j + 1]).then_inc(part_act, 1)
                    if pos % 4 == 1 and unit_in(b, u - 1):
                        U = UB * b + u - 1
                        wait(act, v_ready, U + 1)
                        wait(act, y_ready, U)
                        act.activation(tbuf[:, :], ybuf[:, (u - 1) % 2, :], ACT.Tanh, scale=0.5).then_inc(pre_ready, 1)
                    if pos % 4 == 2 and unit_in(b, u):
                        U = UB * b + u
                        wait(act, fc1_part, 4 * U + 3)
                        wait(act, v_ready, U)
                        act.activation(vhalf[:, :], ypsum[0][:, :], ACT.Copy,
                                       scale=s1c[:, 2 * NJ + j:2 * NJ + j + 1]).then_inc(part_act, 1)
                    due, i = piece_at(b, c, pos, 3)
                    if due:
                        k, cols = w1_pieces[i]
                        act.wait_ge(l_q1[i % 2], 16 * (i // 2 + 1))
                        act.activation(w1[:, k, cols], rin[:, i % 2, :].bitcast(I32), ACT.Copy, bias=-128.0
                                       ).then_inc(w_one, 1)
                    due, i = piece_at(b, c, pos, 4)
                    if due:
                        act.wait_ge(w_raw, i + 1)
                        act.activation(w2h[:, i, :], ybuf[:, i % 2, :], ACT.Copy).then_inc(w_hi, 1)
                    if pos == 0 and chunk_in(b, c):
                        wait(act, s["qT_psum"], g + 1)
                        act.activation(qT[:, :, :].rearrange("p r t -> p (r t)"), bankA[:, :], ACT.Copy
                                       ).then_inc(s["qT_ready"], 1)
                    if pos == 5 and chunk_in(b, c) and c % CB != 0:
                        wait(act, s["inter_psum"], count7(b, c - 1))
                        for half, bank in enumerate((bankA, bankB)):
                            prs = slice(half * PR // 2, (half + 1) * PR // 2)
                            last = act.activation(hint[:, prs, :, :].rearrange("p r e w -> p (r e w)"),
                                                  bank[:, 0:PR * VW], ACT.Copy)
                        last.then_inc(s["hint_raw"], 1)
                    if pos == 10 and chunk_in(b, c - 1):
                        wait(act, s["hT_psum"], g)
                        wait(act, hlo_ready, g - 1)
                        if isinstance(b, int) and g == 1:
                            act.wait_ge(l_bias, 48)
                        act.activation(hstage[:, :, :], bankA[:, :].rearrange("p (k t) -> p k t", t=P), ACT.Copy
                                       ).then_inc(s["hT_ready"], 1)
                    if pos == 11 and chunk_in(b, c - 1):
                        wait(act, s["r_coef"], g)
                        wait(act, s["hn_ready"], g)
                        act.activation(hx[:, :], hx[:, :], ACT.Identity, bias=omv[:, 7:8], scale=omv[:, 6:7]
                                       ).then_inc(s["r_a"], 1)
                    if pos == 11 and chunk_in(b, c - 1):
                        k, n_par = (c - 1) % HC, (c - 1) // HC % 2
                        n = 2 * b + (c - 1) // HC
                        wait(act, s["hT_ready"], g)
                        for kt in range(KT):
                            last = act.activation(hstage[:, kt, :], hstage[:, kt, :], ACT.Identity,
                                                  bias=bcol[:, kt:kt + 1], scale=gcol[:, kt:kt + 1])
                        last.then_inc(s["hg_ready"], 1)
                        wait(act, s["hg_ready"], g)
                        if k == 0:
                            wait(act, fc1_part, 4 * NJ * (n - 1))
                        act.activation(hhi[:, n_par, :, k * P:(k + 1) * P], hstage[:, :, :], ACT.Copy
                                       ).then_inc(hhi_ready, 1)
                    if pos == 13 and chunk_in(b, c):
                        wait(act, s["ex_ready"], g + 1)
                        wait(act, s["hint_ready"], g)
                        wait(act, s["kg_ready"], count7(b, c - 1))
                        act.activation(fac[:, :, :], ex[:, :, :], ACT.Exp).then_inc(s["fac_ready"], 1)
                        wait(act, s["masked"], g + 1)
                        act.activation(dmat[:, :, :, :], dmat[:, :, :, :], ACT.Exp).then_inc(s["d_ready"], 1)
                    if pos % 4 == 2 and unit_in(b, u - 1):
                        U = UB * b + u - 1
                        wait(act, fc2_part, 4 * (U - 3))
                        wait(act, y_ready, U + 1)
                        act.activation(yhi[:, (u - 1) % 4, :], ybuf[:, (u - 1) % 2, :], ACT.Copy
                                       ).then_inc(yhi_ready, 1)
                    if pos == 3 and chunk_in(b, c):
                        wait(act, s["absf"], g + 1)
                        act.activation(gtmp[:, 1, :], ser[:, 0, :], ACT.Exp, scale=-1.0).then_inc(s["e_ready"], 1)

            slots(act, slot)

        @block.vector
        def _(dve):
            def mean_var(src, st, mv, mvs, eps, value, scale=1.0):
                dve.bn_stats(st[:, :], src)
                dve.drain()
                dve.bn_aggr(mv[:, 0:2], st[:, :]).then_inc(mvs, 1)
                wait(dve, mvs, value)
                dve.tensor_scalar(mv[:, 2:3], mv[:, 1:2], LN_EPS, scale, ALU.add, ALU.mult).then_inc(eps, 1)

            def x_stats(b, c):
                g = CB * b + c
                wait(dve, l_x[c % 2], 16 * (4 * b + c // 2 + 1))
                mean_var(xin[:, c % 2, :], xst, xmv, s["x_mv"], s["x_eps"], g + 1, float(DH))

            def q_norm(b, c):
                g = CB * b + c
                wait(dve, s["x_rstd"], g + 1)
                wait(dve, s["qT_psum"], g)
                dve.tensor_scalar(qn[:, :], xin[:, c % 2, :], xmv[:, 0:1], xmv[:, 3:4], ALU.subtract, ALU.mult
                                  ).then_inc(s["qn_ready"], 1)

            dve.memset(ats[:, :].bitcast(F32), 0.0).then_inc(c_dve, 1)
            dve.memset(ex[:, :, :], 0.0).then_inc(c_dve, 1)
            x_stats(0, 0)
            dve.wait_ge(c_sel, 2)
            dve.tensor_copy(sel[:, :], sel32[:, :]).then_inc(c_dve, 1)
            dve.wait_ge(l_const, 64)
            for e in range(2):
                dve.tensor_copy(gbias[:, :].rearrange("p (g e r) -> p g e r", g=2, e=2)[:, :, e, :],
                                gbraw[:, :].rearrange("p (g r e) -> p g r e", g=2, e=2)[:, :, :, e]).then_inc(c_dve, 1)
            dve.tensor_scalar(b2h[:, :], b2h[:, :], 0.5, None, ALU.mult).then_inc(c_dve, 1)
            dve.wait_ge(c_gcopy, 3)
            dve.tensor_tensor(wg[:, KT:2 * KT, :].rearrange("p k h -> p (k h)"),
                              wg[:, KT:2 * KT, :].rearrange("p k h -> p (k h)"),
                              bankA[:, 2 * KT * 2 * NH:3 * KT * 2 * NH], ALU.add).then_inc(c_wg, 1)
            q_norm(0, 0)

            def log1p(value):
                e, zinv, z, z2, acc = gtmp[:, 1, :], ser[:, 0, :], ser[:, 1, :], ser[:, 2, :], ser[:, 3, :]
                wait(dve, s["e_ready"], value)
                dve.tensor_scalar(zinv, e, 2.0, None, ALU.add)
                dve.drain()
                dve.reciprocal(z2, zinv)
                dve.drain()
                dve.tensor_tensor(z, e, z2, ALU.mult)
                dve.drain()
                dve.tensor_tensor(z2, z, z, ALU.mult)
                dve.drain()
                dve.tensor_scalar(acc, z2, ATANH[-1], None, ALU.mult)
                for k in reversed(ATANH[:-1]):
                    dve.drain()
                    dve.scalar_tensor_tensor(out=acc, in0=acc, scalar=k, in1=z2, op0=ALU.add, op1=ALU.mult)
                dve.drain()
                dve.scalar_tensor_tensor(out=acc, in0=acc, scalar=1.0, in1=z, op0=ALU.add, op1=ALU.mult)
                dve.drain()
                dve.scalar_tensor_tensor(out=lf[:, :], in0=acc, scalar=-2.0, in1=gtmp[:, 0, :], op0=ALU.mult,
                                         op1=ALU.add).then_inc(s["lf_ready"], 1)

            def h_of_chunk(v):
                banks = [bank[:, 0:PR * VW].rearrange("p (r w) -> p r w", w=VW) for bank in (bankA, bankB)]
                heads = [slice(e * PR, e * PR + PR) for e in range(2)]
                wait(dve, s["hint_ready"], v)
                wait(dve, s["h_psum"], v)
                for e in range(2):
                    last = dve.tensor_tensor(nrm[:, 1, heads[e]], banks[e][:, :, e * DH], hint[:, :, e, e * DH], ALU.add)
                last.then_inc(s["sum_ready"], 1)
                wait(dve, st_r, 16 * (v - 1))
                for e in range(2):
                    last = dve.tensor_tensor(hv(hx[:, :], e), banks[e][:, :, 1 - e:1 - e + DH],
                                             hint[:, :, e, 1 - e:1 - e + DH], ALU.add)
                last.then_inc(s["h_evac"], 1)
                wait(dve, s["sum_ready"], v)
                dve.scalar_tensor_tensor(out=nrm[:, 0, :], in0=nrm[:, 1, :], scalar=-1.0, in1=fac[:, 3, :],
                                         op0=ALU.mult, op1=ALU.max).then_inc(s["nrm_a"], 1)
                wait(dve, s["nrm_a"], v)
                dve.tensor_tensor(nrm[:, 0, :], nrm[:, 0, :], nrm[:, 1, :], ALU.max).then_inc(s["nrm_b"], 1)
                wait(dve, s["nrm_b"], v)
                dve.tensor_scalar(nrm[:, 0, :], nrm[:, 0, :], NORM_EPS, None, ALU.add).then_inc(s["nrm_c"], 1)
                wait(dve, s["nrm_c"], v)
                dve.reciprocal(nrm[:, 1, :], nrm[:, 0, :]).then_inc(s["rec_ready"], 1)

            def update_state(b, c):
                later = (c - 1) % CB != 0
                if later:
                    wait(dve, s["st_a"], (CB - 2) * (b + (c - 1) // CB) + (c - 1) % CB)
                wait(dve, s["upd_psum"], count7(b, c - 1))
                for e in range(2):
                    ps = slice(e * DH, e * DH + DH)
                    new = bankB[ps, 0:PR * VW].rearrange("p (r w) -> p r w", w=VW)
                    if later:
                        last = dve.tensor_tensor(state[ps, :, e, :], state[ps, :, e, :], new, ALU.add)
                    else:
                        last = dve.tensor_copy(state[ps, :, e, :], new)
                last.then_inc(s["state_ready"], 1)

            def exponents(b, c):
                g, first = CB * b + c, c % CB == 0
                wait(dve, s["abc_psum"], g + 1)
                for e, (bank, done) in enumerate(((bankA, s["argA"]), (bankB, s["argB"]))):
                    bv = bank[:, :].rearrange("p (r t) -> p r t", t=P)
                    hs = slice(e * PR, e * PR + PR)
                    dve.tensor_copy(mnew[:, c % 2, hs], bv[:, :, P - 1])
                    dve.tensor_tensor(dmat[:, e, :, :], acol[:, hs].unsqueeze(2).broadcast_to([P, PR, P]),
                                      bv, ALU.subtract).then_inc(done, 1)
                mprev = minit[:, :] if first else mnew[:, (c + 1) % 2, :]
                wait(dve, s["argB"], g + 1)
                wait(dve, s["an_ready"], g + 1)
                dve.tensor_tensor(ex[:, 0, :], mprev, an[:, :], ALU.subtract)
                dve.tensor_tensor(ex[:, 1, :], acol[:, :], mnew[:, c % 2, :], ALU.subtract)
                for e in range(2):
                    ps, hs = slice(e * DH, e * DH + DH), slice(e * PR, e * PR + PR)
                    dve.tensor_tensor(ex[ps, 2, 0:PR], mprev[ps, hs], mnew[ps, c % 2, hs], ALU.subtract)
                dve.scalar_tensor_tensor(out=ex[:, 3, :], in0=cs[:, :], scalar=-1.0, in1=an[:, :],
                                         op0=ALU.mult, op1=ALU.subtract).then_inc(s["ex_ready"], 1)

            def add_part(b, u, k):
                U, j = UB * b + u, u % NJ
                acc = ybuf[:, u % 2, :] if k == 1 else vhalf[:, :]
                wait(dve, fc1_part, 4 * U + k + 1)
                wait(dve, part_act, 2 * U + (k + 1) // 2)
                dve.scalar_tensor_tensor(out=acc, in0=ypsum[1][:, :], scalar=s1c[:, k * NJ + j:k * NJ + j + 1], in1=acc,
                                         op0=ALU.mult, op1=ALU.add).then_inc(part_dve, 1)

            def two_silu(b, u):
                y = ybuf[:, u % 2, :]
                wait(dve, pre_ready, UB * b + u + 1)
                dve.scalar_tensor_tensor(out=y, in0=tbuf[:, :], scalar=1.0, in1=y, op0=ALU.add, op1=ALU.mult
                                         ).then_inc(y_ready, 1)

            def slot(b, c):
                g = CB * b + c
                first = c % CB == 0
                for pos in range(POS):
                    u = UPS * (c - LAG) + pos // 4
                    if pos % 4 == 1 and unit_in(b, u):
                        add_part(b, u, 1)
                    if pos in (3, 11, 15) and unit_in(b, u):
                        add_part(b, u, 3)
                    if pos == 5 and unit_in(b, u - 1):
                        two_silu(b, u - 1)
                    due, i = piece_at(b, c, pos, 4)
                    if due:
                        wait(dve, l_q2, 16 * (i + 1))
                        wait(dve, l_s2, 16 * (i + 1))
                        wait(dve, w_hi, i - 1)
                        dve.scalar_tensor_tensor(out=ybuf[:, i % 2, :], in0=rin[:, 2, :].bitcast(I32), scalar=-128.0,
                                                 in1=rin[:, 3, :], op0=ALU.add, op1=ALU.mult).then_inc(w_raw, 1)
                    due, i = piece_at(b, c, pos, 6)
                    if due:
                        wait(dve, w_hi, i + 1)
                        dve.tensor_tensor(w2l[:, i, :], ybuf[:, i % 2, :], w2h[:, i, :].bitcast(F32), ALU.subtract
                                          ).then_inc(w_lo, 1)
                        if i == NJ - 1:
                            for m in range(HC):
                                dve.drain().then_inc(rin_left[m], 16)
                    if pos == 0 and chunk_in(b, c):
                        wait(dve, s["kT_psum"], g + 1)
                        dve.tensor_copy(kT[:, :, :].rearrange("p r t -> p (r t)"), bankB[:, :]).then_inc(s["kT_ready"], 1)
                    if pos == 2 and chunk_in(b, c - 1):
                        h_of_chunk(g)
                    if pos == 3 and chunk_in(b, c - 1) and c % CB != 0:
                        update_state(b, c)
                    if pos == 3 and chunk_in(b, c - 1):
                        wait(dve, s["h_ready"], g)
                        mean_var(hx[:, :], hst, hmv, s["h_mv"], s["h_eps"], g)
                    if pos == 3 and chunk_in(b, c):
                        wait(dve, s["gate_psum"], g + 1)
                        dve.tensor_tensor(gate[:, :], bankA[:, 0:2 * NH], gbias[:, :], ALU.add
                                          ).then_inc(s["gate_ready"], 1)
                        wait(dve, s["gate_ready"], g + 1)
                        dve.scalar_tensor_tensor(out=ser[:, 0, :], in0=gate[:, NH:2 * NH], scalar=-1.0,
                                                 in1=gate[:, NH:2 * NH], op0=ALU.mult, op1=ALU.max
                                                 ).then_inc(s["absf"], 1)
                        dve.tensor_scalar(gtmp[:, 0, :], gate[:, NH:2 * NH], 0.0, None, ALU.min)
                    if pos == 4 and chunk_in(b, c - 1):
                        dve.scalar_tensor_tensor(out=hx[:, :], in0=hx[:, :], scalar=hmv[:, 0:1], in1=lnsc[:, :],
                                                 op0=ALU.subtract, op1=ALU.mult).then_inc(s["hs_ready"], 1)
                    if pos == 4 and chunk_in(b, c):
                        log1p(g + 1)
                    if pos == 5 and chunk_in(b, c - 1):
                        wait(dve, s["hs_ready"], g)
                        wait(dve, s["h_rstd"], g)
                        dve.scalar_tensor_tensor(out=hx[:, :], in0=hx[:, :], scalar=hmv[:, 3:4],
                                                 in1=xin[:, (c - 1) % 2, :], op0=ALU.mult, op1=ALU.add
                                                 ).then_inc(s["x1_ready"], 1)
                    if pos == 6 and chunk_in(b, c):
                        wait(dve, s["cs_psum"], g + 1)
                        dve.tensor_copy(cs[:, :], bankA[:, 0:NH])
                        dve.tensor_tensor(acol[:, :], gate[:, 0:NH], bankA[:, 0:NH], ALU.subtract
                                          ).then_inc(s["a_ready"], 1)
                        if first:
                            dve.tensor_copy(lfsum[:, :], lf[:, :]).then_inc(s["lfsum_ready"], 1)
                        else:
                            dve.tensor_tensor(lfsum[:, :], lfsum[:, :], lf[:, :], ALU.add
                                              ).then_inc(s["lfsum_ready"], 1)
                    if pos == 6 and unit_in(b, u):
                        add_part(b, u, 3)
                    if pos == 6 and chunk_in(b, c - 1):
                        wait(dve, s["x1_ready"], g)
                        dve.bn_stats(ost[:, :], hx[:, :])
                        dve.drain()
                        dve.bn_aggr(omv[:, 0:2], ost[:, :]).then_inc(s["o_mv"], 1)
                        wait(dve, s["o_mv"], g)
                        dve.tensor_scalar(omv[:, 2:3], omv[:, 1:2], LN_EPS, None, ALU.add)
                        dve.tensor_scalar(omv[:, 3:4], omv[:, 1:2], 1.0 + LN_EPS, LN_EPS ** 2, ALU.mult, ALU.add
                                          ).then_inc(s["o_eps"], 1)
                    if pos == 8 and chunk_in(b, c):
                        wait(dve, s["aT_psum"], g + 1)
                        init = NEG if first else at[:, (c + 1) % 2, P - 1:P]
                        dve.tensor_tensor_scan(at[:, c % 2, :], bankB[0:NH, 0:P],
                                               minit[0:NH, 0:1].broadcast_to([NH, P]), init, ALU.max,
                                               ALU.max).then_inc(s["at_ready"], 1)
                        wait(dve, s["at_ready"], g + 1)
                        dve.tensor_copy(ats[0:NH, :], at[:, c % 2, :]).then_inc(s["ahi_ready"], 1)
                        wait(dve, s["ahi_ready"], g + 1)
                        dve.tensor_tensor(ats[32:32 + NH, :], at[:, c % 2, :], ats[0:NH, :].bitcast(F32),
                                          ALU.subtract).then_inc(s["ats_ready"], 1)
                    if pos == 8 and chunk_in(b, c - 1):
                        wait(dve, s["o_rstd"], g)
                        dve.tensor_scalar(omv[:, 6:7], omv[:, 4:5], 1.0, None, ALU.add)
                        dve.tensor_scalar(omv[:, 7:8], omv[:, 0:1], omv[:, 4:5], -1.0, ALU.mult, ALU.mult
                                          ).then_inc(s["r_coef"], 1)
                        wait(dve, s["hT_psum"], g - 1)
                        dve.tensor_scalar(hn[:, :], hx[:, :], omv[:, 0:1], omv[:, 5:6], ALU.subtract, ALU.mult
                                          ).then_inc(s["hn_ready"], 1)
                    if pos == 10 and chunk_in(b, c):
                        wait(dve, s["an_psum"], g + 1)
                        dve.tensor_copy(an[:, :], bankB[:, 0:NH]).then_inc(s["an_ready"], 1)
                    if pos == 10 and chunk_in(b, c + 1):
                        x_stats(b, c + 1)
                    if pos == 12 and chunk_in(b, c):
                        exponents(b, c)
                    if pos == 13 and chunk_in(b, c + 1):
                        q_norm(b, c + 1)
                    if pos in (1, 9, 13) and unit_in(b, u - 1):
                        two_silu(b, u - 1)
                    if pos == 13 and chunk_in(b, c - 1):
                        k, n_par = (c - 1) % HC, (c - 1) // HC % 2
                        wait(dve, hhi_ready, g)
                        dve.tensor_tensor(hlo[:, n_par, :, k * P:(k + 1) * P], hstage[:, :, :],
                                          hhi[:, n_par, :, k * P:(k + 1) * P].bitcast(F32), ALU.subtract
                                          ).then_inc(hlo_ready, 1)
                    if pos == 14 and chunk_in(b, c):
                        wait(dve, s["d_ready"], g + 1)
                        wait(dve, s["score_psum"], g + 1)
                        for e, (bank, done) in enumerate(((bankA, s["pA"]), (bankB, s["pB"]))):
                            dv = dmat[:, e, :, :].rearrange("p r t -> p (r t)")
                            dve.tensor_tensor(dv, dv, bank[:, :], ALU.mult).then_inc(done, 1)
                    if pos in Z_POS and c % HC == 1 and unit_in(b, UPS * (c - LAG) - NJ):
                        n = 2 * b + c // HC - 2
                        m = Z_POS.index(pos)
                        wait(dve, l_rin[m], 16 * (n + 1))
                        wait(dve, fc2_part, HC * (NJ * (n + 1) - 1) + m + 1)
                        dve.scalar_tensor_tensor(out=rin[:, m, :], in0=zpsum[m][:, :], scalar=0.25,
                                                 in1=rin[:, m, :], op0=ALU.mult, op1=ALU.add).then_inc(z_free, 1)

            slots(dve, slot)

        @block.tensor
        def _(pe):
            pe.wait_ge(c_ident, 1)
            pe.wait_ge(l_gw, 12 * 16)
            for k in range(3 * KT):
                last = pe.transpose(bankA[:, k * 2 * NH:(k + 1) * 2 * NH], gwraw[k // KT][:, k % KT * P:(k % KT + 1) * P],
                                    ident[0:2 * NH, 0:2 * NH])
            pe.wait_ge(l_s1c, 16)
            pe.transpose(bankB[:, 0:KT * NJ], s1raw, ident[0:KT * NJ, 0:KT * NJ]).then_inc(c_gwT, 1)
            pe.wait_ge(c_ready, 7)
            pe.wait_ge(c_dve, 6)
            pe.wait_ge(c_gcopy, 3)
            pe.wait_ge(c_wg, 1)

            def fc1(b, u, k):
                U, j, n = UB * b + u, u % NJ, 2 * b + u // NJ
                wait(pe, part_act if k % 2 == 0 else part_dve, 2 * U + k // 2)
                if j == 0 and k == 0:
                    if isinstance(U, int) and U == 0:
                        pe.wait_ge(w_one, NJ)
                    wait(pe, hhi_ready, HC * (n + 1))
                    wait(pe, hlo_ready, HC * (n + 1))
                for ht in (hhi, hlo):
                    last = pe.matmul(ypsum[k % 2][:, :], w1[:, k, j * P:(j + 1) * P], ht[:, u // NJ % 2, k, :],
                                     start=ht is hhi, stop=ht is hlo)
                last.then_inc(fc1_part, 1)

            def fc2(b, u, m):
                U, j, n = UB * b + u, u % NJ, 2 * b + u // NJ
                if m == 0:
                    if isinstance(U, int) and U == 0:
                        pe.wait_ge(w_lo, NJ)
                    wait(pe, yhi_ready, U + 1)
                    wait(pe, ylo_ready, U + 1)
                if j == 0:
                    wait(pe, z_free, HC * (n - 1) + m + 1)
                ms = slice(m * P, (m + 1) * P)
                for t, (yt, wt) in enumerate(((yhi, w2h), (yhi, w2l), (ylo, w2h))):
                    last = pe.matmul(zpsum[m][:, :], yt[:, u % 4, ms], wt[:, j, :],
                                     start=(j == 0 and t == 0), stop=(j == NJ - 1 and t == 2))
                last.then_inc(fc2_part, 1)

            def slot(b, c):
                g = CB * b + c
                front, back = chunk_in(b, c), chunk_in(b, c - 1)
                banks = (bankA, bankB)
                for pos in range(POS):
                    u = UPS * (c - LAG) + pos // 4
                    if unit_in(b, u):
                        fc1(b, u, pos % 4)
                    elif front and back:
                        for _ in range(3):
                            pe.matmul(zpsum[0][:, 0:P], ident[:, :], tri[:, :], start=True, stop=True)
                    if unit_in(b, u - 3):
                        fc2(b, u - 3, pos % 4)
                    if pos == 0 and front:
                        wait(pe, s["qn_ready"], g + 1)
                        wait(pe, s["pA"], g)
                        for k in range(KT):
                            last = pe.transpose(bankA[:, k * P:(k + 1) * P], qn[:, k * P:(k + 1) * P], ident[:, :])
                        last.then_inc(s["qT_psum"], 1)
                        wait(pe, l_ctx[c % 2], 16 * (4 * b + c // 2 + 1))
                        wait(pe, s["pB"], g)
                        for k in range(KT):
                            last = pe.transpose(bankB[:, k * P:(k + 1) * P], vaug[:, c % 2, k, 1:1 + P], ident[:, :])
                        last.then_inc(s["kT_psum"], 1)
                    if pos == 1 and back:
                        if front:
                            wait(pe, s["qT_ready"], g + 1)
                            wait(pe, s["kT_ready"], g + 1)
                        wait(pe, s["pA"], g)
                        wait(pe, s["pB"], g)
                        for pr in range(PR):
                            for e, bank in enumerate(banks):
                                last = pe.matmul(bank[:, pr * VW:(pr + 1) * VW], dmat[:, e, pr, :],
                                                 vaug[:, (c - 1) % 2, pr, e * VW:(e + 1) * VW],
                                                 start=True, stop=True)
                        last.then_inc(s["h_psum"], 1)
                    if pos == 3 and back and c % CB != 0:
                        wait(pe, s["h_evac"], g)
                        wait(pe, s["kg_ready"], count7(b, c - 1))
                        for pr in range(PR):
                            for e in range(2):
                                h0 = (2 * pr + e) * DH
                                last = pe.matmul(bankB[e * DH:e * DH + DH, pr * VW:(pr + 1) * VW],
                                                 kg[:, h0:h0 + DH],
                                                 vaug[:, (c - 1) % 2, pr, e * VW:(e + 1) * VW],
                                                 start=True, stop=True)
                        last.then_inc(s["upd_psum"], 1)
                    if pos == 3 and front:
                        wait(pe, s["h_evac"], g)
                        wait(pe, s["qT_ready"], g + 1)
                        wait(pe, s["kT_ready"], g + 1)
                        for k in range(2 * KT):
                            src = qT[:, k, :] if k < KT else kT[:, k - KT, :]
                            last = pe.matmul(bankA[:, 0:2 * NH], src, wg[:, k, :], start=(k == 0),
                                             stop=(k == 2 * KT - 1))
                        last.then_inc(s["gate_psum"], 1)
                    if pos == 5 and front and c % CB != 0:
                        wait(pe, s["gate_ready"], g + 1)
                        wait(pe, s["state_ready"], count7(b, c - 1))
                        for pr in range(PR):
                            k = pr % (PR // 2)
                            last = pe.matmul(banks[pr // (PR // 2)][:, k * 2 * VW:(k + 1) * 2 * VW], qT[:, pr, :],
                                             state[:, pr, :, :].rearrange("p e w -> p (e w)"), start=True, stop=True)
                        last.then_inc(s["inter_psum"], 1)
                    if pos == 6 and front:
                        if c % CB != 0:
                            wait(pe, s["hint_raw"], count7(b, c - 1))
                        wait(pe, s["lf_ready"], g + 1)
                        last = pe.matmul(bankA[:, 0:NH], tri[:, :], lf[:, :], start=True, stop=c % CB == 0)
                        if c % CB != 0:
                            wait(pe, s["lfsum_ready"], g)
                            last = pe.matmul(bankA[:, 0:NH], ones[:, 0:1].broadcast_to([P, P]), lfsum[:, :],
                                             start=False, stop=True)
                        last.then_inc(s["cs_psum"], 1)
                    if pos == 8 and front:
                        wait(pe, s["a_ready"], g + 1)
                        pe.transpose(bankB[0:NH, 0:P], acol[:, :], ident[:, :]).then_inc(s["aT_psum"], 1)
                    if pos == 10 and front:
                        wait(pe, s["at_ready"], g + 1)
                    if pos == 10 and back:
                        wait(pe, s["hn_ready"], g)
                        for k in range(KT):
                            last = pe.transpose(bankA[:, k * P:(k + 1) * P], hn[:, k * P:(k + 1) * P], ident[:, :])
                        last.then_inc(s["hT_psum"], 1)
                    if pos == 10 and front:
                        pe.transpose(bankB[:, 0:NH], at[:, c % 2, :], ident[0:NH, 0:NH]).then_inc(s["an_psum"], 1)
                    if pos == 11 and front:
                        wait(pe, s["hT_ready"], g)
                        wait(pe, s["ats_ready"], g + 1)
                        for e in range(2):
                            if e == 1:
                                wait(pe, s["an_ready"], g + 1)
                            for pr in range(PR):
                                h = e * PR + pr
                                last = pe.matmul(banks[e][:, pr * P:(pr + 1) * P],
                                                 sel[:, h:h + 1].broadcast_to([40, P]), ats[:, :],
                                                 start=True, stop=True)
                        last.then_inc(s["abc_psum"], 1)
                    if pos == 13 and front:
                        wait(pe, s["argA"], g + 1)
                        wait(pe, s["argB"], g + 1)
                        for pr in range(PR):
                            for e, bank in enumerate(banks):
                                ps = slice(e * DH, e * DH + DH)
                                last = pe.matmul(bank[:, pr * P:(pr + 1) * P], kT[ps, pr, :], qT[ps, pr, :],
                                                 start=True, stop=True)
                        last.then_inc(s["score_psum"], 1)

            slots(pe, slot)


_INS = ['x', 'ctx_1024', 'L0_xattn_igate_w', 'L0_xattn_igate_b', 'L0_xattn_fgate_w', 'L0_xattn_fgate_b',
        'L0_xattn_ln_scale', 'L0_ffn_ln_gamma', 'L0_ffn_ln_beta', 'L0_ffn_fc1_q', 'L0_ffn_fc1_scales',
        'L0_ffn_fc1_bias', 'L0_ffn_fc2_q', 'L0_ffn_fc2_scales', 'L0_ffn_fc2_bias']


def kernel(**inputs):
    import numpy as _np
    import concourse.bacc as _bacc
    from concourse import mybir as _mybir
    from concourse.bass_utils import run_bass_kernel_spmd as _run

    nc = _bacc.Bacc("TRN2", target_bir_lowering=False, num_devices=1)
    arrays, args = {}, []
    for name in _INS:
        a = _np.ascontiguousarray(inputs[name])
        arrays[f"in_{name}_dram"] = a
        args.append(nc.dram_tensor(f"in_{name}_dram", a.shape, _mybir.dt.from_np(a.dtype), kind="ExternalInput").ap())
    shape = tuple(inputs['x'].shape)
    args.append(nc.dram_tensor("out_0_dram", shape, F32, kind="ExternalOutput").ap())
    build(nc, *args)
    r = _run(nc, [arrays], core_ids=[0])
    return r.results[0]["out_0_dram"]
```
